# Optimizing a Trainium2 kernel written in Bass

```python
import numpy as np
import jax
import jax.numpy as jnp

def _softmax(x, axis=-1):
    return jax.nn.softmax(x, axis=axis)

def _gelu(x):
    return jax.nn.gelu(x, approximate=True)

def _silu(x):
    return jax.nn.silu(x)

def _sigmoid(x):
    return jax.nn.sigmoid(x)

def _layernorm(x, axis=-1, eps=1e-05):
    m = jnp.mean(x, axis=axis, keepdims=True)
    v = jnp.var(x, axis=axis, keepdims=True)
    return (x - m) / jnp.sqrt(v + eps)

def _scatter_add(tgt, idx, src, axis=0):
    return tgt.at[idx].add(src)

def _segment_sum(src, seg, n):
    return jax.ops.segment_sum(src, seg, n)
kernel_name = 'mk_gnn_preln_d1_gnn_r64_c1d266'

def setup_inputs(seed: int=0):
    np.random.seed(seed)
    _w = jnp.asarray

    def _rec_inputs():
        import jax
        import jax.numpy as jnp
        _gk = jax.random.key(seed)
        x = -0.000202 + 1 * jax.random.normal(jax.random.fold_in(_gk, 1), (100000, 128), jnp.float32)
        _s = jax.random.randint(jax.random.fold_in(_gk, 2), (12500,), 0, 100000, jnp.int32)
        _d = jax.random.randint(jax.random.fold_in(_gk, 3), (12500,), 0, 100000, jnp.int32)
        _loop = jnp.arange(100000, dtype=jnp.int32)
        src = jnp.concatenate([_s, _d, _loop])
        dst = jnp.concatenate([_d, _s, _loop])
        _o = jnp.argsort(dst, stable=True)
        src = src[_o]
        dst = dst[_o]
        return (x, src, dst)
    x, src, dst = _rec_inputs()

    def _L0_gnn_setup():
        import jax, jax.numpy as jnp
        import numpy as np
        N_NODES = 50000
        N_EDGES = 12500
        IN_CH = 128
        OUT_CH = 128
        MLP_HID = 64
        key = jax.random.key(seed)
        ks = jax.random.split(key, 8)
        x = jax.random.normal(ks[0], (N_NODES, IN_CH), dtype=jnp.float32)
        edge_index = jax.random.randint(ks[1], (2, N_EDGES), 0, N_NODES, dtype=jnp.int64)
        s1 = 1.0 / np.sqrt(2 * IN_CH)
        mlp_w1 = jax.random.uniform(ks[2], (2 * IN_CH, MLP_HID), jnp.float32, -s1, s1)
        mlp_b1 = jax.random.uniform(ks[3], (MLP_HID,), jnp.float32, -s1, s1)
        s2 = 1.0 / np.sqrt(MLP_HID)
        mlp_w2 = jax.random.uniform(ks[4], (MLP_HID, 1), jnp.float32, -s2, s2)
        mlp_b2 = jax.random.uniform(ks[5], (1,), jnp.float32, -s2, s2)
        s3 = 1.0 / np.sqrt(IN_CH)
        conv_w = jax.random.uniform(ks[6], (IN_CH, OUT_CH), jnp.float32, -s3, s3)
        conv_b = jnp.zeros((OUT_CH,), jnp.float32)
        return {'x': x, 'edge_index': edge_index, 'mlp_w1': mlp_w1, 'mlp_b1': mlp_b1, 'mlp_w2': mlp_w2, 'mlp_b2': mlp_b2, 'conv_w': conv_w, 'conv_b': conv_b}
    _L0_gnn_all = _L0_gnn_setup()
    _L0_gnn_in = {k: v for k, v in _L0_gnn_all.items() if k in ('mlp_w1', 'mlp_b1', 'mlp_w2', 'mlp_b2', 'conv_w', 'conv_b')}
    del _L0_gnn_all
    return {'x': x, 'src': src, 'dst': dst, 'L0_gnn_mlp_w1': _L0_gnn_in['mlp_w1'], 'L0_gnn_mlp_b1': _L0_gnn_in['mlp_b1'], 'L0_gnn_mlp_w2': _L0_gnn_in['mlp_w2'], 'L0_gnn_mlp_b2': _L0_gnn_in['mlp_b2'], 'L0_gnn_conv_w': _L0_gnn_in['conv_w'], 'L0_gnn_conv_b': _L0_gnn_in['conv_b']}

def reference(x, src, dst, L0_gnn_mlp_w1, L0_gnn_mlp_b1, L0_gnn_mlp_w2, L0_gnn_mlp_b2, L0_gnn_conv_w, L0_gnn_conv_b):
    import jax
    import jax.numpy as jnp

    def _L0_gnn_ref(x, edge_index, mlp_w1, mlp_b1, mlp_w2, mlp_b2, conv_w, conv_b):
        import jax, jax.numpy as jnp
        import numpy as np
        N_NODES = 50000
        N_EDGES = 12500
        IN_CH = 128
        OUT_CH = 128
        MLP_HID = 64
        n = x.shape[0]
        row, col = (edge_index[0], edge_index[1])
        edge_feat = jnp.concatenate([x[row], x[col]], axis=-1)
        h = jax.nn.gelu(edge_feat @ mlp_w1 + mlp_b1, approximate=False)
        edge_weight = jax.nn.sigmoid(h @ mlp_w2 + mlp_b2)[:, 0]
        loop = jnp.arange(n, dtype=row.dtype)
        row_f = jnp.concatenate([row, loop])
        col_f = jnp.concatenate([col, loop])
        ew_f = jnp.concatenate([edge_weight, jnp.ones((n,), x.dtype)])
        deg = jax.ops.segment_sum(ew_f, col_f, num_segments=n)
        dinv = jnp.where(deg > 0, jax.lax.rsqrt(deg), 0.0)
        norm = dinv[row_f] * ew_f * dinv[col_f]
        xt = x @ conv_w
        msg = xt[row_f] * norm[:, None]
        out = jax.ops.segment_sum(msg, col_f, num_segments=n)
        return out + conv_b
    edge_index = jnp.stack([src, dst])
    h = jnp.maximum(_layernorm(x, axis=-1), 0.0)
    x = x + _L0_gnn_ref(h, edge_index, L0_gnn_mlp_w1, L0_gnn_mlp_b1, L0_gnn_mlp_w2, L0_gnn_mlp_b2, L0_gnn_conv_w, L0_gnn_conv_b)
    return x

_drawn_inputs = setup_inputs


def setup_inputs(seed=0):
    import zlib

    import numpy as np

    out = dict(_drawn_inputs(seed))
    spreads = {'L0_gnn_conv_b': (0.0, 0.1)}
    factors = {'L0_gnn_mlp_w1': 8.0, 'L0_gnn_mlp_b1': 63.466, 'L0_gnn_mlp_w2': 8.0}
    for name, (base, spread) in spreads.items():
        noise = np.random.default_rng([zlib.crc32(name.encode()), seed]).standard_normal(out[name].shape)
        drawn = base * np.exp(spread * noise) if base else spread * noise
        out[name] = jnp.asarray(drawn.astype(out[name].dtype))
    for name, factor in factors.items():
        out[name] = (out[name] * factor).astype(out[name].dtype)
    return out
```

```python
from contextlib import ExitStack

import concourse.bass as bass
from concourse import mybir

P = 128
C = 8
HC = C // 2
J = 8
F = 128
HID = 64
BANK = 512
VALUE_BITS = 17
KEY_BASE = 1 << 29
ROUND = 1.5 * (1 << 23)
EPS = 1e-5

ALU = mybir.AluOpType
ACT = mybir.ActivationFunctionType
AX_X = mybir.AxisListType.X
F32 = mybir.dt.float32
BF16 = mybir.dt.bfloat16
F16 = mybir.dt.float16
I32 = mybir.dt.int32
U32 = mybir.dt.uint32


def sizes(n_nodes, n_edges):
    npp = -(-(n_nodes + P + 1) // P)
    npp = -(-npp // (2 * J)) * 2 * J
    epp = -(-(n_edges + 1) // P)
    return npp, epp


def node_index(ap, npp):
    return ap.rearrange("(p j) f -> p j f", j=npp)


def gnn_layer(nc, n_nodes, x, src, dst, w1, b1, w2, b2, conv_w, conv_b, out):
    NP = x.shape[0]
    NPP = NP // P
    NHALF = NPP // 2
    G = NPP // J
    EPP = src.shape[1]
    NB_MAX = -(-EPP // C)
    EW = NB_MAX * C
    CW = EW + 2 * C
    PAD = n_nodes
    PAD_KEY = KEY_BASE | PAD
    assert NP < 1 << VALUE_BITS and NHALF <= BANK and NP >= n_nodes + P + 1 and G >= 8
    assert EPP + 1 < 1 << (29 - VALUE_BITS)

    import numpy as np
    pad_float = float(np.array([PAD_KEY], np.int32).view(np.float32)[0])

    xt_dram = nc.dram_tensor("xt_dram", [NP, F], F32, kind="Internal").ap()
    msg_dram = nc.dram_tensor("msg_dram", [P, CW * F], F32, kind="Internal").ap()
    dinv_dram = nc.dram_tensor("dinv_dram", [NP, 1], F32, kind="Internal").ap()

    x_t = node_index(x, NPP)
    xt_t = node_index(xt_dram, NPP)
    out_t = node_index(out, NPP)

    with ExitStack() as ctx:
        def sb(name, shape, dt=F32):
            return ctx.enter_context(nc.sbuf_tensor(name, shape, dt))

        def sem(name):
            return ctx.enter_context(nc.semaphore(name))

        ps_t = ctx.enter_context(nc.psum_tensor("ps_t", [P, 2, BANK], F32))
        ps_hid = ctx.enter_context(nc.psum_tensor("ps_hid", [P, 2, BANK], F32))
        ps_xt = ctx.enter_context(nc.psum_tensor("ps_xt", [P, 2, BANK], F32))
        ps_deg = ctx.enter_context(nc.psum_tensor("ps_deg", [P, 2, BANK], F32))

        ident = sb("ident", [P, P])
        ones = sb("ones", [P, P])
        lower = sb("lower", [P, P])
        trash = sb("trash", [P, 1])
        trash_i = sb("trash_i", [P, 1], I32)
        hi_iota_i = sb("hi_iota_i", [P, P], I32)
        hi_iota = sb("hi_iota", [P, P], BF16)
        lo_iota_i = sb("lo_iota_i", [P, NPP], I32)
        lo_iota = sb("lo_iota", [P, NPP], F16)
        zeros16 = sb("zeros16", [P, BANK], BF16)
        w1_sb = sb("w1_sb", [P, 2, HID])
        w1_sum = sb("w1_sum", [P, HID])
        conv_sb = sb("conv_sb", [P, F])
        b1_row = sb("b1_row", [1, J, HID])
        w2_all = sb("w2_all", [P, HID])
        b2_all = sb("b2_all", [P, 1])
        b2_half = sb("b2_half", [P, 1])
        cb_all = sb("cb_all", [P, F])
        pow_exp = sb("pow_exp", [P, J])

        src_i = sb("src_i", [P, EPP], I32)
        dst_i = sb("dst_i", [P, EPP], I32)
        src_f = sb("src_f", [P, EPP])
        dst_f = sb("dst_f", [P, EPP])
        loop_dst = sb("loop_dst", [P, EPP])
        highest = sb("highest", [P, EPP + 1])
        canon = sb("canon", [P, EPP])
        n_canon = sb("n_canon", [P, 2])
        row2 = sb("row2", [1, 2, P])
        carry = sb("carry", [P, 1])
        all_canon = sb("all_canon", [P, 1])
        extra = sb("extra", [P, EPP], U32)
        n_extra = sb("n_extra", [P, 1])
        most = sb("most", [1, 2])
        n_blocks_i = sb("n_blocks_i", [1, 2], I32)
        pos_key = sb("pos_key", [P, EPP], I32)
        full_key = sb("full_key", [P, EPP], I32)
        src_key = sb("src_key", [P, EW])
        dst_key = sb("dst_key", [P, EW])
        best = sb("best", [P, 2, C])
        src_col = sb("src_col", [P, CW], I32)
        dst_col = sb("dst_col", [P, CW], I32)
        gather_idx = sb("gather_idx", [P, 2, 2 * HC], I32)

        xin = sb("xin", [P, 2, J, F])
        xn = sb("xn", [P, 2, J, F])
        hT = sb("hT", [P, 2, J, F])
        gel = sb("gel", [P, 2, J, HID])
        xout = sb("xout", [P, 2, J, F])
        stats = sb("stats", [P, 2, J, 6])
        m_sum = sb("m_sum", [P, 2, J])
        m_dif = sb("m_dif", [P, 2, J])
        m2 = sb("m2", [P, 2, J])
        mean = sb("mean", [P, 2, J])
        var = sb("var", [P, 2, J])
        rstd = sb("rstd", [P, 2, J])
        logit = sb("logit", [P, 2, HC])
        w_col = sb("w_col", [P, 2, HC])
        w_16 = sb("w_16", [P, 2, HC], BF16)
        w_rest = sb("w_rest", [P, 3, HC])
        d_f = sb("d_f", [P, C])
        d_q = sb("d_q", [P, C])
        d_r = sb("d_r", [P, C])
        d_hi = sb("d_hi", [P, C])
        d_lo = sb("d_lo", [P, C])
        hot_hi = sb("hot_hi", [P, 2, 3, P], BF16)
        hot_lo = sb("hot_lo", [P, 2, NPP], BF16)

        node_z = sb("node_z", [P, NPP])
        deg = sb("deg", [P, NPP])
        dinv = sb("dinv", [P, NPP])
        coef = sb("coef", [P, NPP])
        t_a = sb("t_a", [P, NPP])
        t_b = sb("t_b", [P, NPP])

        dinv_idx = sb("dinv_idx", [P, 2, C], I32)
        dinv_g = sb("dinv_g", [P, 2, C])
        scale = sb("scale", [P, C])
        dcol_f = sb("dcol_f", [P, C])
        msg = sb("msg", [P, C, F])
        msg_s = sb("msg_s", [P, C, F])
        same = sb("same", [P, 2, P])
        same_low = sb("same_low", [P, P])
        prior = sb("prior", [P, C])
        to_trash = sb("to_trash", [P, C])
        row_f = sb("row_f", [P, C])
        row_col = sb("row_col", [P, CW], I32)
        row_idx = sb("row_idx", [P, C], I32)
        merged = sb("merged", [P, C, F])

        edges_loaded = sem("edges_loaded")
        weights_loaded = sem("weights_loaded")
        pool_const = sem("pool_const")
        consts_ready = sem("consts_ready")
        prep_vec = sem("prep_vec")
        prep_stat = sem("prep_stat")
        prep_pe = sem("prep_pe")
        carry_ready = sem("carry_ready")
        blocks_known = sem("blocks_known")

        sorted_block = sem("sorted_block")
        sort_vec = sem("sort_vec")
        idx_copied = sem("idx_copied")
        waited = sem("waited")
        gathered = [sem(f"gathered{h}") for h in range(2)]
        a_vec = sem("a_vec")
        a_norm = sem("a_norm")
        a_turned = sem("a_turned")
        a_relu = sem("a_relu")
        a_hid = sem("a_hid")
        a_xt = sem("a_xt")
        a_gelu = sem("a_gelu")
        a_logit = sem("a_logit")
        a_tanh = sem("a_tanh")
        a_w = sem("a_w")
        a_msg = sem("a_msg")
        a_stored = [sem(f"a_stored{h}") for h in range(2)]
        a_hot = sem("a_hot")
        a_deg = sem("a_deg")
        a_xout = sem("a_xout")
        deg_all = sem("deg_all")
        edges_deg = sem("edges_deg")

        n_loaded = [sem(f"n_loaded{s}") for s in range(2)]
        n_vec = sem("n_vec")
        n_b2 = sem("n_b2")
        n_scaled = sem("n_scaled")
        n_var = sem("n_var")
        n_rstd = sem("n_rstd")
        n_norm = sem("n_norm")
        n_turned = sem("n_turned")
        n_relu = sem("n_relu")
        n_mm = sem("n_mm")
        n_gelu = sem("n_gelu")
        n_prod = sem("n_prod")
        n_xt_a = sem("n_xt_a")
        n_xt_v = sem("n_xt_v")
        n_stored = [sem(f"n_stored{s}") for s in range(2)]
        nodes_z = sem("nodes_z")

        c_tanh = sem("c_tanh")
        c_vec = sem("c_vec")
        c_deg = sem("c_deg")
        c_sqrt = sem("c_sqrt")
        c_dinv = sem("c_dinv")
        c_coef = sem("c_coef")
        dinv_stored = sem("dinv_stored")

        b_x = [sem(f"b_x{s}") for s in range(2)]
        b_xt = [sem(f"b_xt{s}") for s in range(2)]
        b_bias = sem("b_bias")
        b_out = sem("b_out")
        b_stored = [sem(f"b_stored{s}") for s in range(2)]

        s_idx = sem("s_idx")
        s_dinv = sem("s_dinv")
        s_vec = sem("s_vec")
        s_scale = sem("s_scale")
        s_msg_in = sem("s_msg_in")
        s_msg = sem("s_msg")
        s_dst = sem("s_dst")
        s_row_idx = sem("s_row_idx")
        s_turned = sem("s_turned")
        s_same = sem("s_same")
        s_sum = sem("s_sum")
        s_merged = sem("s_merged")
        s_row = sem("s_row")
        s_added = sem("s_added")
        s_landed = sem("s_landed")

        block = ctx.enter_context(nc.Block())

        def load_blocks(eng):
            eng.wait_ge(blocks_known, 1)
            return eng.value_load(n_blocks_i[0:1, 0:1], min_val=1, max_val=NB_MAX)

        def pipeline(eng, stages):
            last = max(lag for _, lag in stages)
            lead = -(-(last + 2) // 2) * 2

            def step(turn, u, at=None):
                for f, lag in stages:
                    if at is not None and not 0 <= at - lag < G:
                        continue
                    v = u - lag
                    f(turn * 2 + v, v % 2, turn + v // 2, at is None or at - lag >= 2)

            for s in range(lead):
                step(s // 2, s % 2, s)
            with eng.Fori(lead // 2, G // 2) as turn:
                for u in range(2):
                    step(turn, u)
            for s in range(G, G + last):
                step(s // 2, s % 2, s)

        CREDIT = 2

        @block.sync
        def _(sp):
            sp.dma_start(src_i[:], src).then_inc(edges_loaded, 16)
            sp.dma_start(dst_i[:], dst).then_inc(edges_loaded, 16)
            sp.dma_start(w1_sb[:], w1.rearrange("(t p) h -> p t h", p=P)).then_inc(weights_loaded, 16)
            sp.dma_start(conv_sb[:], conv_w).then_inc(weights_loaded, 16)
            sp.dma_start(b1_row[:], b1.unsqueeze(1).to_broadcast([1, J, HID])).then_inc(weights_loaded, 16)
            sp.dma_start(w2_all[:], w2.to_broadcast([P, HID])).then_inc(weights_loaded, 16)
            sp.dma_start(b2_all[:], b2.to_broadcast([P, 1])).then_inc(weights_loaded, 16)
            sp.dma_start(cb_all[:], conv_b.to_broadcast([P, F])).then_inc(weights_loaded, 16)

            nb = load_blocks(sp)
            with sp.Fori(0, nb) as b:
                for h in range(2):
                    sp.wait_ge(a_msg, b * 2 + (h + 1 + CREDIT))
                    sp.dma_start(msg_dram[:, bass.ds(b * (C * F) + h * HC * F, HC * F)],
                                 xout[:, h, 0:HC, :].rearrange("p c f -> p (c f)")).then_inc(a_stored[h], 16)
                    sp.wait_ge(a_stored[h], b * 16 + 16)
                    sp.sem_inc(a_xout, 1)
            sp.wait_ge(edges_deg, 1)

            def load_x(g, s, r, again):
                if again:
                    sp.wait_ge(n_norm, g - 1)
                sp.dma_start(xin[:, s], x_t[:, bass.ds(g * J, J), :]).then_inc(n_loaded[s], 16)

            def store_xt(g, s, r, again):
                sp.wait_ge(n_xt_a, g + 1)
                sp.wait_ge(n_xt_v, g + 1)
                sp.dma_start(xt_t[:, bass.ds(g * J, J), :], xout[:, s]).then_inc(n_stored[s], 16)

            pipeline(sp, [(load_x, 0), (store_xt, 3)])

            sp.wait_ge(c_dinv, 1)
            sp.dma_start(dinv_dram.rearrange("(p j) o -> p (j o)", j=NPP), dinv[:]).then_inc(dinv_stored, 16)
            for s in range(2):
                sp.wait_ge(n_stored[s], 16 * (G // 2))
            sp.wait_ge(n_turned, 2 * G)

            def load_base(g, s, r, again):
                if again:
                    sp.wait_ge(b_out, g - 1)
                sp.dma_start(xin[:, s], x_t[:, bass.ds(g * J, J), :]).then_inc(b_x[s], 16)
                sp.dma_start(xn[:, s], xt_t[:, bass.ds(g * J, J), :]).then_inc(b_xt[s], 16)

            def store_base(g, s, r, again):
                sp.wait_ge(b_out, g + 1)
                sp.dma_start(out_t[:, bass.ds(g * J, J), :], xout[:, s]).then_inc(b_stored[s], 16)

            pipeline(sp, [(load_base, 0), (store_base, 1)])

            with sp.Fori(0, nb) as b:
                sp.wait_ge(s_msg, b + 1)
                sp.dma_start(msg[:].rearrange("p c f -> p (c f)"),
                             msg_dram[:, bass.ds(b * (C * F), C * F)]).then_inc(s_msg_in, 16)

        @block.gpsimd
        def _(pool):
            pool.memset(ones[:], 1.0).then_inc(pool_const, 1)
            pool.wait_ge(pool_const, 1)
            pool.affine_select(out=ident[:], in_=ones[:], compare_op=ALU.is_equal, fill=0.0, base=0,
                               pattern=[[-1, P]], channel_multiplier=1).then_inc(pool_const, 1)
            pool.affine_select(out=lower[:], in_=ones[:], compare_op=ALU.is_gt, fill=0.0, base=0,
                               pattern=[[-1, P]], channel_multiplier=1).then_inc(pool_const, 1)
            pool.iota(trash_i[:], pattern=[[0, 1]], base=n_nodes + 1, channel_multiplier=1).then_inc(pool_const, 1)
            pool.iota(hi_iota_i[:], pattern=[[1, P]], base=0, channel_multiplier=0).then_inc(pool_const, 1)
            pool.iota(lo_iota_i[:], pattern=[[1, NPP]], base=0, channel_multiplier=0).then_inc(pool_const, 1)
            pool.iota(pos_key[:], pattern=[[-1, EPP]], base=(KEY_BASE >> VALUE_BITS) + EPP,
                      channel_multiplier=0).then_inc(pool_const, 1)
            pool.memset(zeros16[:], 0.0).then_inc(pool_const, 1)
            pool.memset(pow_exp[:], -0.5).then_inc(pool_const, 1)
            pool.memset(src_key[:].bitcast(I32), PAD_KEY).then_inc(pool_const, 1)
            pool.memset(dst_key[:].bitcast(I32), PAD_KEY).then_inc(pool_const, 1)

            nb = load_blocks(pool)

            def held():
                pool.sem_inc(waited, 1)

            def gather_half(b, h):
                pool.wait_ge(sorted_block, b + 1)
                pool.wait_ge(a_norm, b * 2 + (h + 1))
                at = b * C + h * HC
                pool.tensor_copy(gather_idx[:, h, 0:HC], src_col[:, bass.ds(at, HC)]).then_inc(idx_copied, 1)
                pool.tensor_copy(gather_idx[:, h, HC:], dst_col[:, bass.ds(at, HC)]).then_inc(idx_copied, 1)
                pool.wait_ge(idx_copied, b * 4 + (h * 2 + 2))
                held()
                for c in range(2 * HC):
                    pool.indirect_dma_start(xin[:, h, c, :], None, x, bass.IndirectOffsetOnAxis(
                        ap=gather_idx[:, h, c:c + 1], axis=0)).then_inc(gathered[h], 16)

            gather_half(0, 0)
            with pool.Fori(0, nb) as b:
                gather_half(b, 1)
                gather_half(b + 1, 0)

            def power(g, s, r, again):
                if again:
                    pool.wait_ge(n_norm, g - 1)
                pool.wait_ge(n_var, g + 1)
                pool.tensor_tensor(rstd[:, s, :], var[:, s, :], pow_exp[:], ALU.pow).then_inc(n_rstd, 1)

            pipeline(pool, [(power, 0)])

            def add_bias(g, s, r, again):
                pool.wait_ge(b_x[s], r * 16 + 16)
                pool.tensor_tensor(xin[:, s], xin[:, s], cb_all[:].unsqueeze(1).to_broadcast([P, J, F]),
                                   ALU.add).then_inc(b_bias, 1)

            pipeline(pool, [(add_bias, 0)])

            def dinv_indices(b):
                pool.wait_ge(s_scale, b + 1)
                at = b * C
                pool.tensor_copy(dinv_idx[:, 0, :], src_col[:, bass.ds(at, C)]).then_inc(s_idx, 1)
                pool.tensor_copy(dinv_idx[:, 1, :], dst_col[:, bass.ds(at, C)]).then_inc(s_idx, 1)
                pool.wait_ge(s_idx, b * 2 + 2)
                held()

            def dinv_gathers(c):
                for k in range(2):
                    pool.indirect_dma_start(dinv_g[:, k, c:c + 1], None, dinv_dram, bass.IndirectOffsetOnAxis(
                        ap=dinv_idx[:, k, c:c + 1], axis=0)).then_inc(s_dinv, 16)

            pool.wait_ge(dinv_stored, 16)
            dinv_indices(0)
            for c in range(C):
                dinv_gathers(c)
            for s in range(2):
                pool.wait_ge(b_stored[s], 16 * (G // 2))
            with pool.Fori(0, nb) as b:
                dinv_indices(b + 1)
                pool.wait_ge(s_row, b + 2)
                pool.tensor_copy(row_idx[:], row_col[:, bass.ds(b * C, C)]).then_inc(s_row_idx, 1)
                for c in range(C):
                    if c == 0:
                        pool.wait_ge(s_row_idx, b + 1)
                    pool.wait_ge(s_merged, b * C + (c + 3))
                    held()
                    pool.indirect_dma_start(out, bass.IndirectOffsetOnAxis(ap=row_idx[:, c:c + 1], axis=0),
                                            merged[:, c, :], None, compute_op=ALU.add).then_inc(s_added, 16)
                    dinv_gathers(c)
                    pool.wait_ge(s_added, b * (16 * C) + 16 * (c + 1))
                pool.sem_inc(s_landed, 1)
            pool.wait_ge(s_dinv, nb * (16 * 2 * C) + 16 * 2 * C)

        @block.tensor
        def _(pe):
            pe.wait_ge(pool_const, 11)
            pe.wait_ge(prep_stat, 1)
            pe.transpose(ps_t[0:2, 0, 0:P], n_canon[:], ident[:]).then_inc(prep_pe, 1)
            pe.wait_ge(carry_ready, 1)
            pe.transpose(ps_t[:, 1, 0:1], row2[0:1, 0, :], ident[0:1, 0:1]).then_inc(prep_pe, 1)
            pe.wait_ge(prep_stat, 2)
            pe.matmul(ps_hid[:, 0, 0:1], ones[:], n_canon[:, 1:2], start=True, stop=True).then_inc(prep_pe, 1)
            pe.wait_ge(prep_stat, 3)
            pe.transpose(ps_t[0:1, 0, 0:P], n_extra[:], ident[:]).then_inc(prep_pe, 1)

            for k in range(2):
                pe.matmul(ps_deg[:, k, 0:NHALF], zeros16[:, 0:P], zeros16[:, 0:NHALF], start=True, stop=False)
            nb = load_blocks(pe)
            pe.wait_ge(weights_loaded, 16 * 6)
            with pe.Fori(0, nb) as b:
                for h in range(2):
                    pe.wait_ge(a_norm, b * 2 + (h + 1 + CREDIT))
                    for k in range(2):
                        pe.wait_ge(a_relu, b * 4 + (2 * h + k + 1))
                        for c in range(HC):
                            mm = pe.transpose(ps_t[:, k, c * P:(c + 1) * P], xn[:, h, k * HC + c, :], ident[:])
                        mm.then_inc(a_turned, 1)
                    pe.wait_ge(a_gelu, b * 2 + (h + 1))
                    pe.matmul(ps_hid[:, h, 0:HC * HID], ones[0:1, :], b1_row[:, 0:HC, :], start=True, stop=False,
                              skip_group_check=True)
                    pe.wait_ge(a_relu, b * 4 + (2 * h + 2 + 2))
                    for c in range(HC):
                        for k in range(2):
                            mm = pe.matmul(ps_hid[:, h, c * HID:(c + 1) * HID], hT[:, h, k * HC + c, :],
                                           w1_sb[:, k, :], start=False, stop=(k == 1 and c == HC - 1),
                                           skip_group_check=True)
                    mm.then_inc(a_hid, 1)
                    pe.wait_ge(a_msg, b * 2 + (h + 1))
                    for c in range(HC):
                        mm = pe.matmul(ps_xt[:, h, c * F:(c + 1) * F], hT[:, h, c, :], conv_sb[:],
                                       start=True, stop=True)
                    mm.then_inc(a_xt, 1)
                for q in range(C):
                    pe.wait_ge(a_hot, b * C + (q + 1))
                    for part in range(3):
                        for k in range(2):
                            mm = pe.matmul(ps_deg[:, k, 0:NHALF], hot_hi[:, q % 2, part, :],
                                           hot_lo[:, q % 2, k * NHALF:(k + 1) * NHALF], start=False, stop=False)
                    mm.then_inc(a_deg, 1)
            for k in range(2):
                mm = pe.matmul(ps_deg[:, k, 0:NHALF], zeros16[:, 0:P], zeros16[:, 0:NHALF], start=False, stop=True)
            mm.then_inc(deg_all, 1)

            pe.wait_ge(edges_deg, 1)

            def xt_bank(s, k):
                return ps_deg[:, k] if s else ps_xt[:, k]

            def turn(g, s, r, again):
                pe.wait_ge(n_norm, g + 1)
                for k in range(2):
                    if again or g >= 1:
                        pe.wait_ge(n_relu, g * 2 + (k - 1))
                    for c in range(J // 2):
                        mm = pe.transpose(ps_t[:, k, c * P:(c + 1) * P], xn[:, s, k * (J // 2) + c, :], ident[:])
                    mm.then_inc(n_turned, 1)

            def multiply(g, s, r, again):
                pe.wait_ge(n_relu, g * 2 + 2)
                if again:
                    pe.wait_ge(n_gelu, g - 1)
                pe.matmul(ps_hid[:, s, :], ones[0:1, :], b1_row[:].rearrange("o j h -> o (j h)"),
                          start=True, stop=False, skip_group_check=True)
                for c in range(J):
                    mm = pe.matmul(ps_hid[:, s, c * HID:(c + 1) * HID], hT[:, s, c, :], w1_sum[:],
                                   start=False, stop=(c == J - 1), skip_group_check=True)
                mm.then_inc(n_mm, 1)
                if again:
                    pe.wait_ge(n_xt_a, g - 1)
                    pe.wait_ge(n_xt_v, g - 1)
                for c in range(J):
                    at = c % (J // 2) * F
                    mm = pe.matmul(xt_bank(s, c // (J // 2))[:, at:at + F], hT[:, s, c, :], conv_sb[:],
                                   start=True, stop=True)
                mm.then_inc(n_mm, 1)

            pipeline(pe, [(turn, 0), (multiply, 1)])

            def merge(b, c):
                pe.wait_ge(s_same, b * C + (c + 1 + 2))
                pe.wait_ge(s_merged, b * C + (c + 1))
                pe.matmul(ps_hid[:, c % 2, 0:F], same[:, c % 2, :], msg_s[:, c, :],
                          start=True, stop=True).then_inc(s_sum, 1)

            with pe.Fori(0, nb) as b:
                pe.wait_ge(s_dst, b + 1)
                for c in range(C):
                    pe.wait_ge(s_same, b * C + (c + 1))
                    pe.transpose(ps_t[:, c % 2, 0:P], dcol_f[:, c:c + 1].to_broadcast([P, P]),
                                 ident[:]).then_inc(s_turned, 1)
                    if c == 0:
                        pe.wait_ge(s_msg, b + 2)
                    if c >= 1:
                        merge(b, c - 1)
                merge(b, C - 1)

        @block.scalar
        def _(act):
            act.wait_ge(weights_loaded, 16 * 6)
            act.mul(b2_half[:], b2_all[:], 0.5).then_inc(n_b2, 1)
            act.wait_ge(n_b2, 1)
            nb = load_blocks(act)
            with act.Fori(0, nb) as b:
                for h in range(2):
                    act.wait_ge(a_xt, b * 2 + (h + 1))
                    for k in range(2):
                        act.wait_ge(a_turned, b * 4 + (2 * h + k + 1 + 2 * CREDIT))
                        act.activation(hT[:, h, k * HC:(k + 1) * HC, :].rearrange("p c f -> p (c f)"),
                                       ps_t[:, k, :], ACT.Relu).then_inc(a_relu, 1)
                    act.wait_ge(a_hid, b * 2 + (h + 1))
                    act.wait_ge(a_logit, b * 2 + (h + 1))
                    act.activation(gel[:, h, 0:HC, :].rearrange("p c f -> p (c f)"),
                                   ps_hid[:, h, 0:HC * HID], ACT.Gelu).then_inc(a_gelu, 1)
                    act.wait_ge(a_logit, b * 2 + (h + 1 + CREDIT))
                    act.activation(w_col[:, h, :], logit[:, h, :], ACT.Tanh, bias=b2_half[:],
                                   scale=0.5).then_inc(a_tanh, 1)
                    act.wait_ge(a_w, b * 2 + (h + 1))
                    act.wait_ge(a_xt, b * 2 + (h + 1 + CREDIT))
                    act.wait_ge(a_xout, b * 2 + (h + 1))
                    for c in range(HC):
                        mm = act.activation(xout[:, h, c, :], ps_xt[:, h, c * F:(c + 1) * F], ACT.Copy,
                                            scale=w_col[:, h, c:c + 1])
                    mm.then_inc(a_msg, 1)
            for h in range(2):
                act.wait_ge(a_stored[h], nb * 16)
            act.wait_ge(edges_deg, 1)

            def relu(g, s, r, again):
                if again:
                    act.wait_ge(n_mm, g * 2 - 2)
                for k in range(2):
                    act.wait_ge(n_turned, g * 2 + (k + 1))
                    act.activation(hT[:, s, k * (J // 2):(k + 1) * (J // 2), :].rearrange("p c f -> p (c f)"),
                                   ps_t[:, k, :], ACT.Relu).then_inc(n_relu, 1)

            def gelu(g, s, r, again):
                act.wait_ge(n_mm, g * 2 + 1)
                if again:
                    act.wait_ge(n_prod, g - 1)
                act.activation(gel[:, s].rearrange("p c f -> p (c f)"), ps_hid[:, s, :],
                               ACT.Gelu).then_inc(n_gelu, 1)

            def xt_out(g, s, r, again):
                act.wait_ge(n_mm, g * 2 + 2)
                if again:
                    act.wait_ge(n_stored[s], r * 16)
                bank = ps_deg[:, 0] if s else ps_xt[:, 0]
                act.activation(xout[:, s, 0:J // 2, :].rearrange("p c f -> p (c f)"), bank,
                               ACT.Copy).then_inc(n_xt_a, 1)

            pipeline(act, [(relu, 0), (gelu, 1), (xt_out, 1)])

            act.wait_ge(nodes_z, 1)
            act.activation(node_z[:], node_z[:], ACT.Tanh, bias=b2_half[:], scale=0.5).then_inc(c_tanh, 1)
            act.wait_ge(c_deg, 1)
            act.activation(t_b[:], deg[:], ACT.Sqrt).then_inc(c_sqrt, 1)

            with act.Fori(0, nb) as b:
                act.wait_ge(s_scale, b + 2)
                act.wait_ge(s_msg_in, b * 16 + 16)
                act.wait_ge(s_sum, b * C + 2)
                for c in range(C):
                    mm = act.activation(msg_s[:, c, :], msg[:, c, :], ACT.Copy, scale=scale[:, c:c + 1])
                mm.then_inc(s_msg, 1)
                for c in range(C):
                    act.wait_ge(s_sum, b * C + (c + 3))
                    if c == 0:
                        act.wait_ge(s_landed, b + 1)
                    act.activation(merged[:, c, :], ps_hid[:, c % 2, 0:F], ACT.Copy).then_inc(s_merged, 1)

        @block.vector
        def _(dve):
            def chain(semaphore, base=0):
                count = [0]

                def link(ins):
                    count[0] += 1
                    ins.then_inc(semaphore, 1)
                    dve.wait_ge(semaphore, base + count[0])
                return link, count

            link, _ = chain(prep_vec)
            dve.memset(highest[:, 0:1], 0.0)
            for s, n in ((a_norm, CREDIT), (a_turned, 2 * CREDIT), (a_relu, 2), (a_gelu, CREDIT), (a_xt, CREDIT),
                         (a_msg, CREDIT), (a_logit, CREDIT), (a_xout, CREDIT), (s_landed, 1), (s_row, 1), (a_deg, 2),
                         (s_scale, 1), (s_msg, 1), (s_same, 2), (s_merged, 2), (s_sum, 2), (s_turned, 1)):
                dve.sem_inc(s, n)
            dve.wait_ge(edges_loaded, 32)
            dve.tensor_copy(src_f[:], src_i[:])
            link(dve.tensor_copy(dst_f[:], dst_i[:]))
            link(dve.tensor_tensor(canon[:], src_f[:], dst_f[:], ALU.is_equal))
            link(dve.scalar_tensor_tensor(loop_dst[:], dst_f[:], 1.0, canon[:], ALU.add, ALU.mult))
            link(dve.tensor_tensor_scan(highest[:, 1:], loop_dst[:], loop_dst[:], 0.0, ALU.max, ALU.max))
            dve.tensor_copy(n_canon[:, 1:2], highest[:, EPP:EPP + 1])
            dve.tensor_copy(n_canon[:, 0:1], highest[:, EPP:EPP + 1]).then_inc(prep_stat, 1)
            dve.wait_ge(prep_pe, 1)
            link(dve.tensor_copy(row2[0:1, 1, :], ps_t[0:1, 0, 0:P]))
            dve.memset(row2[0:1, 0, 0:1], 0.0)
            dve.tensor_tensor_scan(row2[0:1, 0, 1:P], row2[0:1, 1, 0:P - 1], row2[0:1, 1, 0:P - 1], 0.0,
                                   ALU.max, ALU.max).then_inc(carry_ready, 1)
            dve.wait_ge(prep_pe, 2)
            link(dve.tensor_copy(carry[:], ps_t[:, 1, 0:1]))
            link(dve.scalar_tensor_tensor(canon[:], highest[:, 0:EPP], carry[:], loop_dst[:], ALU.max, ALU.is_lt))
            dve.reduce_sum(n_canon[:, 1:2], canon[:], AX_X).then_inc(prep_stat, 1)
            dve.wait_ge(prep_pe, 3)
            link(dve.tensor_scalar(all_canon[:], ps_hid[:, 0, 0:1], float(n_nodes + 1), None, ALU.is_equal))
            dve.wait_ge(pool_const, 11)
            link(dve.tensor_scalar(extra[:], canon[:], all_canon[:], 0.0, ALU.mult, ALU.is_equal))
            link(dve.tensor_copy(canon[:], extra[:]))
            dve.reduce_sum(n_extra[:], canon[:], AX_X).then_inc(prep_stat, 1)
            link(dve.tensor_scalar(pos_key[:], pos_key[:], VALUE_BITS, None, ALU.logical_shift_left))
            for key, node in ((src_key, src_i), (dst_key, dst_i)):
                link(dve.tensor_tensor(full_key[:], pos_key[:], node[:], ALU.bitwise_or))
                link(dve.copy_predicated(key[:, 0:EPP].bitcast(I32), extra[:], full_key[:]))
            dve.wait_ge(prep_pe, 4)
            link(dve.reduce_max(most[:, 0:1], ps_t[0:1, 0, 0:P], AX_X))
            link(dve.tensor_scalar(n_blocks_i[:, 1:2], most[:, 0:1], float(C - 1), None, ALU.add))
            dve.tensor_scalar(n_blocks_i[:, 0:1], n_blocks_i[:, 1:2], C.bit_length() - 1, None,
                              ALU.logical_shift_right).then_inc(blocks_known, 1)
            dve.tensor_copy(hi_iota[:], hi_iota_i[:])
            dve.tensor_copy(lo_iota[:], lo_iota_i[:])
            dve.tensor_copy(trash[:], trash_i[:])
            dve.wait_ge(weights_loaded, 16 * 6)
            link(dve.tensor_tensor(w1_sum[:], w1_sb[:, 0, :], w1_sb[:, 1, :], ALU.add))

            nb = load_blocks(dve)

            SORT_STEPS = 2

            def sort_block(b):
                dve.max(best[:, 0, :], src_key[:])
                dve.max(best[:, 1, :], dst_key[:]).then_inc(sort_vec, 1)
                dve.wait_ge(sort_vec, b * SORT_STEPS + 1)
                mask = (1 << VALUE_BITS) - 1
                dve.tensor_scalar(src_col[:, bass.ds(b * C, C)], best[:, 0, :].bitcast(I32), mask, None,
                                  ALU.bitwise_and)
                dve.tensor_scalar(dst_col[:, bass.ds(b * C, C)], best[:, 1, :].bitcast(I32), mask, None,
                                  ALU.bitwise_and).then_inc(sorted_block, 1)
                dve.match_replace(src_key[:], best[:, 0, :], src_key[:], pad_float)
                dve.match_replace(dst_key[:], best[:, 1, :], dst_key[:], pad_float).then_inc(sort_vec, 1)
                dve.wait_ge(sort_vec, b * SORT_STEPS + 2)

            def moments(s, link):
                for c in range(J):
                    last = dve.bn_stats(stats[:, s, c, :], xin[:, s, c, :])
                link(last)
                dve.tensor_tensor(m_sum[:, s, :], stats[:, s, :, 1], stats[:, s, :, 4], ALU.add)
                dve.tensor_tensor(m2[:, s, :], stats[:, s, :, 2], stats[:, s, :, 5], ALU.add)
                link(dve.tensor_tensor(m_dif[:, s, :], stats[:, s, :, 1], stats[:, s, :, 4], ALU.subtract))
                dve.tensor_scalar(mean[:, s, :], m_sum[:, s, :], 0.5, None, ALU.mult)
                link(dve.tensor_tensor(m_dif[:, s, :], m_dif[:, s, :], m_dif[:, s, :], ALU.mult))
                link(dve.scalar_tensor_tensor(m2[:, s, :], m_dif[:, s, :], F / 4.0, m2[:, s, :], ALU.mult, ALU.add))
                return dve.tensor_scalar(var[:, s, :], m2[:, s, :], 1.0 / F, EPS, ALU.mult, ALU.add)

            def normalise(s):
                for c in range(J):
                    last = dve.tensor_scalar(xn[:, s, c, :], xin[:, s, c, :], mean[:, s, c:c + 1],
                                             rstd[:, s, c:c + 1], ALU.subtract, ALU.mult)
                return last

            LN_LINKS = 16

            def ln_half(b, h, base):
                link, n = chain(a_vec, base)
                dve.wait_ge(gathered[h], b * (16 * 2 * HC) + 16 * 2 * HC)
                link(moments(h, link))
                y, v, t = rstd[:, h, :], var[:, h, :], m_dif[:, h, :]
                link(dve.tensor_scalar(y.bitcast(I32), v.bitcast(I32), 1, None, ALU.logical_shift_right))
                dve.tensor_scalar(v, v, -0.5, None, ALU.mult)
                link(dve.tensor_scalar(y.bitcast(I32), y.bitcast(I32), -1.0, float(0x5F3759DF), ALU.mult, ALU.add))
                for _ in range(3):
                    link(dve.tensor_tensor(t, y, y, ALU.mult))
                    link(dve.tensor_tensor(t, t, v, ALU.mult))
                    link(dve.scalar_tensor_tensor(y, t, 1.5, y, ALU.add, ALU.mult))
                dve.wait_ge(a_turned, b * 4 + (2 * h + 2))
                normalise(h).then_inc(a_norm, 1)
                assert n[0] == LN_LINKS, n[0]

            POST_LINKS = 10

            def post_half(b, h, base):
                link, n = chain(a_vec, base)
                half = b * 2 + h
                dve.wait_ge(a_gelu, half + (1 + CREDIT))
                link(dve.tensor_tensor(gel[:, h, 0:HC, :], gel[:, h, 0:HC, :],
                                       w2_all[:].unsqueeze(1).to_broadcast([P, HC, HID]), ALU.mult))
                dve.reduce_sum(logit[:, h, :], gel[:, h, 0:HC, :], AX_X).then_inc(a_logit, 1)
                cols = slice(0, HC)
                link(dve.tensor_copy(d_f[:, cols], dst_col[:, bass.ds(b * C + h * HC, HC)]))
                link(dve.tensor_scalar(d_q[:, cols], d_f[:, cols], 1.0 / NPP, 0.5 / NPP - 0.5, ALU.mult, ALU.add))
                link(dve.tensor_scalar(d_r[:, cols], d_q[:, cols], ROUND, None, ALU.add))
                link(dve.tensor_scalar(d_hi[:, cols], d_r[:, cols], ROUND, None, ALU.subtract))
                dve.scalar_tensor_tensor(d_lo[:, cols], d_hi[:, cols], -float(NPP), d_f[:, cols], ALU.mult, ALU.add)
                dve.wait_ge(a_tanh, half + 1)
                link(dve.tensor_scalar(w_rest[:, 0, :], w_col[:, h, :], 0.5, 0.5, ALU.mult, ALU.add))
                dve.tensor_copy(w_col[:, h, :], w_rest[:, 0, :]).then_inc(a_w, 1)
                for k in range(2):
                    link(dve.tensor_copy(w_16[:, k, :], w_rest[:, k, :]))
                    link(dve.tensor_tensor(w_rest[:, k + 1, :], w_rest[:, k, :], w_16[:, k, :], ALU.subtract))
                for c in range(HC):
                    q = half * HC + c
                    dve.wait_ge(a_deg, q + 1)
                    for k in range(3):
                        dve.tensor_scalar(hot_hi[:, c % 2, k, :], hi_iota[:], d_hi[:, c:c + 1],
                                          w_rest[:, k, c:c + 1], ALU.is_equal, ALU.mult)
                    dve.tensor_scalar(hot_lo[:, c % 2, :], lo_iota[:], d_lo[:, c:c + 1], None,
                                      ALU.is_equal).then_inc(a_hot, 1)
                assert n[0] == POST_LINKS, n[0]

            sort_block(0)
            ln_half(0, 0, 0)
            PER_BLOCK = 2 * (LN_LINKS + POST_LINKS)
            with dve.Fori(0, nb) as b:
                at = b * PER_BLOCK + LN_LINKS
                sort_block(b + 1)
                ln_half(b, 1, at)
                post_half(b, 0, at + LN_LINKS)
                ln_half(b + 1, 0, at + LN_LINKS + POST_LINKS)
                post_half(b, 1, at + 2 * LN_LINKS + POST_LINKS)
            dve.wait_ge(deg_all, 1)
            for k in range(2):
                last = dve.tensor_copy(deg[:, k * NHALF:(k + 1) * NHALF], ps_deg[:, k, 0:NHALF])
            last.then_inc(edges_deg, 1)
            dve.wait_ge(a_stored[0], nb * 16)
            dve.wait_ge(a_stored[1], nb * 16)

            NODE_LINKS = 4

            def node_moments(g, s, r, again):
                link, n = chain(n_vec, g * NODE_LINKS)
                dve.wait_ge(n_loaded[s], r * 16 + 16)
                moments(s, link).then_inc(n_var, 1)
                assert n[0] == NODE_LINKS, n[0]

            def node_norm(g, s, r, again):
                dve.wait_ge(n_rstd, g + 1)
                if again:
                    dve.wait_ge(n_turned, g * 2 - 2)
                normalise(s).then_inc(n_norm, 1)

            def node_xt(g, s, r, again):
                dve.wait_ge(n_mm, g * 2 + 2)
                if again:
                    dve.wait_ge(n_stored[s], r * 16)
                bank = ps_deg[:, 1] if s else ps_xt[:, 1]
                dve.tensor_copy(xout[:, s, J // 2:, :].rearrange("p c f -> p (c f)"), bank).then_inc(n_xt_v, 1)

            def node_logit(g, s, r, again):
                dve.wait_ge(n_gelu, g + 1)
                dve.tensor_tensor(gel[:, s], gel[:, s], w2_all[:].unsqueeze(1).to_broadcast([P, J, HID]),
                                  ALU.mult).then_inc(n_scaled, 1)
                dve.wait_ge(n_scaled, g + 1)
                dve.reduce_sum(node_z[:, bass.ds(g * J, J)], gel[:, s], AX_X).then_inc(n_prod, 1)

            pipeline(dve, [(node_moments, 0), (node_norm, 1), (node_xt, 2), (node_logit, 2)])

            link, _ = chain(c_vec)
            dve.wait_ge(n_prod, G)

            dve.sem_inc(nodes_z, 1)
            dve.wait_ge(c_tanh, 1)
            link(dve.tensor_scalar(t_a[:], node_z[:], 0.5, 0.5, ALU.mult, ALU.add))
            link(dve.tensor_scalar(t_a[:], t_a[:], all_canon[:], 1.0, ALU.mult, ALU.add))
            dve.tensor_tensor(deg[:], deg[:], t_a[:], ALU.add).then_inc(c_deg, 1)
            dve.wait_ge(c_sqrt, 1)
            link(dve.reciprocal(dinv[:], t_b[:]))
            link(dve.tensor_tensor(t_b[:], dinv[:], dinv[:], ALU.mult))
            link(dve.tensor_tensor(t_b[:], t_b[:], deg[:], ALU.mult))
            link(dve.tensor_scalar(t_b[:], t_b[:], -0.5, 1.5, ALU.mult, ALU.add))
            link(dve.tensor_tensor(dinv[:], dinv[:], t_b[:], ALU.mult))
            link(dve.scalar_tensor_tensor(dinv[:], deg[:], 0.0, dinv[:], ALU.is_gt, ALU.mult))
            link(dve.tensor_tensor(coef[:], dinv[:], dinv[:], ALU.mult))
            link(dve.tensor_tensor(coef[:], coef[:], t_a[:], ALU.mult))
            dve.sem_inc(c_dinv, 1)

            def base(g, s, r, again):
                dve.wait_ge(b_bias, g + 1)
                dve.wait_ge(b_xt[s], r * 16 + 16)
                if again:
                    dve.wait_ge(b_stored[s], r * 16)
                for c in range(J):
                    last = dve.scalar_tensor_tensor(xout[:, s, c, :], xn[:, s, c, :],
                                                    coef[:, bass.ds(g * J + c, 1)], xin[:, s, c, :],
                                                    ALU.mult, ALU.add)
                last.then_inc(b_out, 1)

            pipeline(dve, [(base, 0)])

            S_LINKS = 3
            with dve.Fori(0, nb) as b:
                link, n = chain(s_vec, b * S_LINKS)
                dve.wait_ge(s_turned, b * C + 1)
                dve.wait_ge(s_row, b + 1)
                dve.tensor_copy(dcol_f[:], dst_col[:, bass.ds(b * C, C)]).then_inc(s_dst, 1)
                dve.wait_ge(s_dinv, b * (16 * 2 * C) + 16 * 2 * C)
                dve.wait_ge(s_msg, b + 1)
                dve.tensor_tensor(scale[:], dinv_g[:, 0, :], dinv_g[:, 1, :], ALU.mult).then_inc(s_scale, 1)
                for c in range(C):
                    dve.wait_ge(s_turned, b * C + (c + 2))
                    dve.wait_ge(s_sum, b * C + (c + 1))
                    dve.tensor_scalar(same[:, c % 2, :], ps_t[:, c % 2, 0:P], dcol_f[:, c:c + 1], None,
                                      ALU.is_equal).then_inc(s_same, 1)
                    dve.wait_ge(s_same, b * C + (c + 3))
                    last = dve.tensor_tensor_reduce(same_low[:], same[:, c % 2, :], lower[:], 1.0, 0.0, ALU.mult,
                                                    ALU.add, prior[:, c:c + 1])
                link(last)
                link(dve.tensor_scalar(to_trash[:], dcol_f[:], -1.0, trash[:], ALU.mult, ALU.add))
                link(dve.scalar_tensor_tensor(row_f[:], prior[:], 0.0, to_trash[:], ALU.is_gt, ALU.mult))
                dve.tensor_tensor(row_col[:, bass.ds(b * C, C)], row_f[:], dcol_f[:], ALU.add).then_inc(s_row, 1)
                assert n[0] == S_LINKS


def kernel(x, src, dst, L0_gnn_mlp_w1, L0_gnn_mlp_b1, L0_gnn_mlp_w2, L0_gnn_mlp_b2, L0_gnn_conv_w, L0_gnn_conv_b):
    import numpy as np
    import concourse.bacc as bacc
    from concourse.bass_utils import run_bass_kernel_spmd

    x = np.asarray(x)
    n_nodes, n_edges = x.shape[0], np.asarray(src).shape[0]
    npp, epp = sizes(n_nodes, n_edges)
    arrays = {
        "x": np.zeros((P * npp, F), np.float32),
        "src": np.full(P * epp, n_nodes, np.int32),
        "dst": np.full(P * epp, n_nodes, np.int32),
    }
    arrays["x"][:n_nodes] = x
    arrays["src"][:n_edges] = np.asarray(src)
    arrays["dst"][:n_edges] = np.asarray(dst)
    arrays["src"] = arrays["src"].reshape(P, epp)
    arrays["dst"] = arrays["dst"].reshape(P, epp)
    arrays["w1"] = np.ascontiguousarray(L0_gnn_mlp_w1)
    arrays["b1"] = np.asarray(L0_gnn_mlp_b1).reshape(1, HID)
    arrays["w2"] = np.asarray(L0_gnn_mlp_w2).reshape(1, HID)
    arrays["b2"] = np.asarray(L0_gnn_mlp_b2).reshape(1, 1)
    arrays["conv_w"] = np.ascontiguousarray(L0_gnn_conv_w)
    arrays["conv_b"] = np.asarray(L0_gnn_conv_b).reshape(1, F)

    nc = bacc.Bacc("TRN2", target_bir_lowering=False, num_devices=1)
    aps = [nc.dram_tensor(f"in_{n}", a.shape, mybir.dt.from_np(a.dtype), kind="ExternalInput").ap()
           for n, a in arrays.items()]
    out = nc.dram_tensor("out", (P * npp, F), F32, kind="ExternalOutput").ap()
    gnn_layer(nc, n_nodes, *aps, out)
    r = run_bass_kernel_spmd(nc, [{f"in_{n}": a for n, a in arrays.items()}], core_ids=[0])
    return r.results[0]["out"][:n_nodes]
```

```python
from contextlib import ExitStack

import concourse.bass as bass
from concourse import mybir

P = 128
C = 8
HC = C // 2
T = 2
E = 4
MAX_LEAD = 3
J = 8
HJ = J // 2
R = 7
F = 128
HID = 64
BANK = 512
VALUE_BITS = 17
KEY_BASE = 1 << 29
W_SCALE = 4096.0
ROUND = 1.5 * (1 << 23)
EPS = 1e-5

ALU = mybir.AluOpType
ACT = mybir.ActivationFunctionType
AX_X = mybir.AxisListType.X
F32 = mybir.dt.float32
BF16 = mybir.dt.bfloat16
F16 = mybir.dt.float16
I32 = mybir.dt.int32
U32 = mybir.dt.uint32


def sizes(n_nodes, n_edges):
    npp = -(-(n_nodes + P + 1) // P)
    npp = -(-npp // (R * J)) * R * J
    epp = -(-(n_edges + 1) // P)
    return npp, epp


def node_index(ap, npp):
    return ap.rearrange("(p j) f -> p j f", j=npp)


def gnn_layer(nc, n_nodes, x, src, dst, w1, b1, w2, b2, conv_w, conv_b, out):
    NP = x.shape[0]
    NPP = NP // P
    NHALF = NPP // 2
    G = NPP // J
    EPP = src.shape[1]
    NT_MAX = -(-EPP // (T * C))
    EW = NT_MAX * T * C
    CW = EW + MAX_LEAD * C
    PAD = n_nodes
    PAD_KEY = KEY_BASE | PAD
    assert NP < 1 << VALUE_BITS and NHALF <= BANK and NP >= n_nodes + P + 1
    assert EPP + 1 < 1 << (29 - VALUE_BITS)

    import numpy as np
    pad_float = float(np.array([PAD_KEY], np.int32).view(np.float32)[0])

    msg_dram = nc.dram_tensor("msg_dram", [P, CW * F], F32, kind="Internal").ap()
    dinv_dram = nc.dram_tensor("dinv_dram", [NP, 1], F32, kind="Internal").ap()

    x_t = node_index(x, NPP)
    out_t = node_index(out, NPP)

    with ExitStack() as ctx:
        def sb(name, shape, dt=F32):
            return ctx.enter_context(nc.sbuf_tensor(name, shape, dt))

        def sem(name):
            return ctx.enter_context(nc.semaphore(name))

        ps_t = ctx.enter_context(nc.psum_tensor("ps_t", [P, 2, BANK], F32))
        ps_hid = ctx.enter_context(nc.psum_tensor("ps_hid", [P, 2, BANK], F32))
        ps_xt = ctx.enter_context(nc.psum_tensor("ps_xt", [P, 2, BANK], F32))
        ps_deg = ctx.enter_context(nc.psum_tensor("ps_deg", [P, 2, BANK], F32))

        ps_z = ps_xt[:, 1]

        ident = sb("ident", [P, P])
        ones = sb("ones", [P, P])
        lower = sb("lower", [P, P])
        trash = sb("trash", [P, 1])
        trash_i = sb("trash_i", [P, 1], I32)
        hi_iota_i = sb("hi_iota_i", [P, P], I32)
        hi_iota = sb("hi_iota", [P, P], F16)
        lo_iota_i = sb("lo_iota_i", [P, NPP], I32)
        lo_iota = sb("lo_iota", [P, NPP], F16)
        zeros16 = sb("zeros16", [P, BANK], F16)
        w1_sb = sb("w1_sb", [P, 2, HID])
        w1_sum = sb("w1_sum", [P, HID])
        conv_sb = sb("conv_sb", [P, F])
        b1_col = sb("b1_col", [HID, 1])
        w2_col = sb("w2_col", [HID, 1])
        b2_all = sb("b2_all", [P, 1])
        b2_half = sb("b2_half", [P, 1])
        cb_all = sb("cb_all", [P, F])
        half_canon = sb("half_canon", [P, 1])
        half_canon1 = sb("half_canon1", [P, 1])
        gelu_warm = sb("gelu_warm", [P, 1])
        pow_exp = sb("pow_exp", [P, J])

        src_i = sb("src_i", [P, EPP], I32)
        dst_i = sb("dst_i", [P, EPP], I32)
        src_f = sb("src_f", [P, EPP])
        dst_f = sb("dst_f", [P, EPP])
        loop_dst = sb("loop_dst", [P, EPP])
        highest = sb("highest", [P, EPP + 1])
        canon = sb("canon", [P, EPP])
        n_canon = sb("n_canon", [P, 2])
        row2 = sb("row2", [1, 2, P])
        carry = sb("carry", [P, 1])
        all_canon = sb("all_canon", [P, 1])
        extra = sb("extra", [P, EPP], U32)
        n_extra = sb("n_extra", [P, 1])
        most = sb("most", [1, 2])
        n_turns_i = sb("n_turns_i", [1, 2], I32)
        pos_key = sb("pos_key", [P, EPP], I32)
        full_key = sb("full_key", [P, EPP], I32)
        src_key = sb("src_key", [P, EW])
        dst_key = sb("dst_key", [P, EW])
        best = sb("best", [P, 2, C])
        src_col = sb("src_col", [P, CW], I32)
        dst_col = sb("dst_col", [P, CW], I32)
        gather_idx = sb("gather_idx", [P, E, 2 * HC], I32)

        xin = sb("xin", [P, R, J, F])
        xn = sb("xn", [P, R, J, F])
        gel = sb("gel", [HID, 2, BANK])
        xmsg = sb("xmsg", [P, 2, HC, F])
        stats = sb("stats", [P, R, J, 6])
        m_sum = sb("m_sum", [P, R, J])
        m_dif = sb("m_dif", [P, R, J])
        m2 = sb("m2", [P, R, J])
        neg_mean = sb("neg_mean", [P, R, J])
        var = sb("var", [P, R, J])
        rstd = sb("rstd", [P, R, J])
        shift = sb("shift", [P, R, J])
        w_tanh = sb("w_tanh", [P, 2, HC])
        w_col = sb("w_col", [P, 2, HC])
        w_16 = sb("w_16", [P, HC], F16)
        w_part = sb("w_part", [P, 2, HC])
        d_f = sb("d_f", [P, C])
        d_q = sb("d_q", [P, C])
        d_r = sb("d_r", [P, C])
        hi_col = sb("hi_col", [P, CW])
        lo_col = sb("lo_col", [P, CW])
        hot_hi = sb("hot_hi", [P, HC, 2, P], F16)
        hot_lo = sb("hot_lo", [P, HC, NPP], F16)

        node_tanh = sb("node_tanh", [P, R, J])
        self_w = sb("self_w", [P, R, J])
        deg_rec = sb("deg_rec", [P, R, J])
        coef = sb("coef", [P, R, J])
        deg = sb("deg", [P, NPP])
        dinv = sb("dinv", [P, NPP])
        t_b = sb("t_b", [P, NPP])

        dinv_idx = sb("dinv_idx", [P, T, 2, C], I32)
        dinv_g = sb("dinv_g", [P, T, 2, C])
        scale = sb("scale", [P, T, C])
        dcol_f = sb("dcol_f", [P, C])
        msg = sb("msg", [P, C, F])
        msg_s = sb("msg_s", [P, C, F])
        same = sb("same", [P, 2, P])
        same_low = sb("same_low", [P, P])
        prior = sb("prior", [P, C])
        to_trash = sb("to_trash", [P, C])
        row_f = sb("row_f", [P, C])
        row_col = sb("row_col", [P, CW], I32)
        row_idx = sb("row_idx", [P, C], I32)
        merged = sb("merged", [P, T, C, F])

        edges_loaded = sem("edges_loaded")
        weights_loaded = sem("weights_loaded")
        pool_const = sem("pool_const")
        consts_ready = sem("consts_ready")
        prep_vec = sem("prep_vec")
        prep_stat = sem("prep_stat")
        prep_pe = sem("prep_pe")
        carry_ready = sem("carry_ready")
        turns_known = sem("turns_known")

        sorted_block = sem("sorted_block")
        sort_vec = sem("sort_vec")
        idx_copied = sem("idx_copied")
        waited = sem("waited")
        gathered = [sem(f"gathered{h}") for h in range(E)]
        a_ln = sem("a_ln")
        a_post = sem("a_post")
        a_rstd = sem("a_rstd")
        a_norm = sem("a_norm")
        a_turned = sem("a_turned")
        a_evac = sem("a_evac")
        a_hid = sem("a_hid")
        a_gelu = sem("a_gelu")
        a_z = sem("a_z")
        a_tanh = sem("a_tanh")
        a_w = sem("a_w")
        a_xt = sem("a_xt")
        a_msg = sem("a_msg")
        a_stored = [sem(f"a_stored{h}") for h in range(2)]
        a_hot = sem("a_hot")
        a_deg = sem("a_deg")
        a_xout = sem("a_xout")
        deg_all = sem("deg_all")
        edges_deg = sem("edges_deg")

        n_loaded = [sem(f"n_loaded{s}") for s in range(R)]
        n_vec = sem("n_vec")
        n_warm = sem("n_warm")
        n_var = sem("n_var")
        n_pow = sem("n_pow")
        n_rstd = sem("n_rstd")
        n_norm = sem("n_norm")
        n_bias = sem("n_bias")
        n_turned = sem("n_turned")
        n_evac = sem("n_evac")
        n_hid = sem("n_hid")
        n_gelu = sem("n_gelu")
        n_z = sem("n_z")
        n_tanh = sem("n_tanh")
        n_xt = sem("n_xt")
        n_coef = sem("n_coef")
        n_out = sem("n_out")
        n_stored = [sem(f"n_stored{s}") for s in range(R)]

        c_vec = sem("c_vec")
        c_deg = sem("c_deg")
        c_sqrt = sem("c_sqrt")
        c_dinv = sem("c_dinv")
        dinv_stored = sem("dinv_stored")

        s_idx = sem("s_idx")
        s_dinv = [sem(f"s_dinv{t}") for t in range(T)]
        s_vec = sem("s_vec")
        s_scale = sem("s_scale")
        s_msg_in = sem("s_msg_in")
        s_msg = sem("s_msg")
        s_dst = sem("s_dst")
        s_row_idx = sem("s_row_idx")
        s_turned = sem("s_turned")
        s_same = sem("s_same")
        s_sum = sem("s_sum")
        s_merged = sem("s_merged")
        s_row = sem("s_row")
        s_added = sem("s_added")
        s_landed = sem("s_landed")

        block = ctx.enter_context(nc.Block())

        def load_turns(eng):
            eng.wait_ge(turns_known, 1)
            return eng.value_load(n_turns_i[0:1, 0:1], min_val=1, max_val=NT_MAX)

        def pipeline(eng, stages):
            last = max(lag for _, lag in stages)
            lead = -(-(last + R) // R) * R
            assert G >= lead

            def step(turn, u, at=None):
                for f, lag in stages:
                    if at is not None and not 0 <= at - lag < G:
                        continue
                    v = u - lag
                    f(turn * R + v, v % R, turn + v // R, at is None or at - lag >= R)

            for s in range(lead):
                step(s // R, s % R, s)
            with eng.Fori(lead // R, G // R) as turn:
                for u in range(R):
                    step(turn, u)
            for s in range(G, G + last):
                step(s // R, s % R, s)

        credits = ((a_norm, E), (a_rstd, 2), (a_turned, 4), (a_evac, 4), (a_hid, 2), (a_gelu, 2), (a_z, 2),
                   (a_tanh, 2), (a_w, 2), (a_xt, 2), (a_msg, 2), (a_xout, 2), (a_deg, C),
                   (s_landed, T), (s_row, 1), (s_msg, T), (s_same, 2), (s_merged, 2), (s_sum, 2), (s_turned, 1))

        def done(half, n=1, i=0):
            return half * n + (2 * n + i + 1)

        def norm_done(half):
            return half + (E + 1)

        def edge_steps(eng, nt, step):
            step(0, 0)
            with eng.Fori(0, nt) as turn:
                for j in range(1, E + 1):
                    step(turn, j)

        @block.sync
        def _(sp):
            sp.dma_start(src_i[:], src).then_inc(edges_loaded, 16)
            sp.dma_start(dst_i[:], dst).then_inc(edges_loaded, 16)
            sp.dma_start(w1_sb[:], w1.rearrange("(t p) h -> p t h", p=P)).then_inc(weights_loaded, 16)
            sp.dma_start(conv_sb[:], conv_w).then_inc(weights_loaded, 16)
            sp.dma_start(b1_col[:], b1).then_inc(weights_loaded, 16)
            sp.dma_start(w2_col[:], w2).then_inc(weights_loaded, 16)
            sp.dma_start(b2_all[:], b2.to_broadcast([P, 1])).then_inc(weights_loaded, 16)
            sp.dma_start(cb_all[:], conv_b.to_broadcast([P, F])).then_inc(weights_loaded, 16)

            nt = load_turns(sp)
            with sp.Fori(0, nt) as turn:
                for j in range(E):
                    H = turn * E + j
                    sp.wait_ge(a_msg, done(H))
                    sp.dma_start(msg_dram[:, bass.ds(H * (HC * F), HC * F)],
                                 xmsg[:, j % 2, :, :].rearrange("p c f -> p (c f)")).then_inc(a_stored[j % 2], 16)
                    sp.wait_ge(a_stored[j % 2], turn * (16 * E // 2) + 16 * (j // 2 + 1))
                    sp.sem_inc(a_xout, 1)
            sp.wait_ge(edges_deg, 1)

            def load_x(g, s, r, again):
                if again:
                    sp.wait_ge(n_stored[s], r * 16)
                sp.dma_start(xin[:, s], x_t[:, bass.ds(g * J, J), :]).then_inc(n_loaded[s], 16)

            def store_out(g, s, r, again):
                sp.wait_ge(n_out, g * 2 + 2)
                sp.dma_start(out_t[:, bass.ds(g * J, J), :], xin[:, s]).then_inc(n_stored[s], 16)

            pipeline(sp, [(load_x, 0), (store_out, R - 1)])

            sp.wait_ge(c_dinv, 1)
            sp.dma_start(dinv_dram.rearrange("(p j) o -> p (j o)", j=NPP), dinv[:]).then_inc(dinv_stored, 16)
            sp.wait_ge(edges_deg, 1)

            with sp.Fori(0, nt) as turn:
                for t in range(T):
                    b = turn * T + t
                    sp.wait_ge(s_msg, b + T)
                    sp.dma_start(msg[:].rearrange("p c f -> p (c f)"),
                                 msg_dram[:, bass.ds(b * (C * F), C * F)]).then_inc(s_msg_in, 16)

        @block.gpsimd
        def _(pool):
            pool.memset(ones[:], 1.0).then_inc(pool_const, 1)
            pool.wait_ge(pool_const, 1)
            pool.affine_select(out=ident[:], in_=ones[:], compare_op=ALU.is_equal, fill=0.0, base=0,
                               pattern=[[-1, P]], channel_multiplier=1).then_inc(pool_const, 1)
            pool.affine_select(out=lower[:], in_=ones[:], compare_op=ALU.is_gt, fill=0.0, base=0,
                               pattern=[[-1, P]], channel_multiplier=1).then_inc(pool_const, 1)
            pool.iota(trash_i[:], pattern=[[0, 1]], base=n_nodes + 1, channel_multiplier=1).then_inc(pool_const, 1)
            pool.iota(hi_iota_i[:], pattern=[[1, P]], base=0, channel_multiplier=0).then_inc(pool_const, 1)
            pool.iota(lo_iota_i[:], pattern=[[1, NPP]], base=0, channel_multiplier=0).then_inc(pool_const, 1)
            pool.iota(pos_key[:], pattern=[[-1, EPP]], base=(KEY_BASE >> VALUE_BITS) + EPP,
                      channel_multiplier=0).then_inc(pool_const, 1)
            pool.memset(zeros16[:], 0.0).then_inc(pool_const, 1)
            pool.memset(pow_exp[:], -0.5).then_inc(pool_const, 1)
            pool.memset(src_key[:].bitcast(I32), PAD_KEY).then_inc(pool_const, 1)
            pool.memset(dst_key[:].bitcast(I32), PAD_KEY).then_inc(pool_const, 1)

            nt = load_turns(pool)

            def held():
                pool.sem_inc(waited, 1)

            def gather_half(turn, j):
                H = turn * E + j
                slot = j % E
                pool.wait_ge(sorted_block, turn * T + (j // 2 + 1))
                pool.wait_ge(a_norm, norm_done(H - E))
                pool.tensor_copy(gather_idx[:, slot, 0:HC], src_col[:, bass.ds(H * HC, HC)]).then_inc(idx_copied, 1)
                pool.tensor_copy(gather_idx[:, slot, HC:], dst_col[:, bass.ds(H * HC, HC)]).then_inc(idx_copied, 1)
                pool.wait_ge(idx_copied, H * 2 + 2)
                held()
                for c in range(2 * HC):
                    pool.indirect_dma_start(xin[:, slot, c, :], None, x, bass.IndirectOffsetOnAxis(
                        ap=gather_idx[:, slot, c:c + 1], axis=0)).then_inc(gathered[slot], 16)

            gather_half(0, 0)
            gather_half(0, 1)
            with pool.Fori(0, nt) as turn:
                for j in range(2, E + 2):
                    gather_half(turn, j)

            def add_bias(g, s, r, again):
                pool.wait_ge(n_norm, g + 1)
                pool.tensor_tensor(xin[:, s], xin[:, s], cb_all[:].unsqueeze(1).to_broadcast([P, J, F]),
                                   ALU.add).then_inc(n_bias, 1)

            def power(g, s, r, again):
                pool.wait_ge(n_var, g + 1)
                pool.tensor_tensor(rstd[:, s, :], var[:, s, :], pow_exp[:], ALU.pow).then_inc(n_pow, 1)
                pool.wait_ge(n_pow, g + 1)
                pool.tensor_tensor(shift[:, s, :], neg_mean[:, s, :], rstd[:, s, :], ALU.mult).then_inc(n_rstd, 1)

            pipeline(pool, [(power, 0), (add_bias, 3)])

            def dinv_indices(t, b):
                at = b * C
                pool.tensor_copy(dinv_idx[:, t, 0, :], src_col[:, bass.ds(at, C)]).then_inc(s_idx, 1)
                pool.tensor_copy(dinv_idx[:, t, 1, :], dst_col[:, bass.ds(at, C)]).then_inc(s_idx, 1)
                pool.wait_ge(s_idx, b * 2 + 2)
                held()

            def dinv_gathers(t, c):
                for k in range(2):
                    pool.indirect_dma_start(dinv_g[:, t, k, c:c + 1], None, dinv_dram, bass.IndirectOffsetOnAxis(
                        ap=dinv_idx[:, t, k, c:c + 1], axis=0)).then_inc(s_dinv[t], 16)

            pool.wait_ge(dinv_stored, 16)
            for t in range(T):
                dinv_indices(t, t)
                for c in range(C):
                    dinv_gathers(t, c)
            for s in range(R):
                pool.wait_ge(n_stored[s], 16 * (G // R))
            with pool.Fori(0, nt) as turn:
                for t in range(T):
                    b = turn * T + t
                    pool.wait_ge(s_scale, b + 1)
                    dinv_indices(t, b + T)
                    pool.wait_ge(s_row, b + 2)
                    pool.tensor_copy(row_idx[:], row_col[:, bass.ds(b * C, C)]).then_inc(s_row_idx, 1)
                    for c in range(C):
                        if c == 0:
                            pool.wait_ge(s_row_idx, b + 1)
                        pool.wait_ge(s_merged, b * C + (c + 3))
                        held()
                        pool.indirect_dma_start(out, bass.IndirectOffsetOnAxis(ap=row_idx[:, c:c + 1], axis=0),
                                                merged[:, t, c, :], None, compute_op=ALU.add).then_inc(s_added, 16)
                        dinv_gathers(t, c)
                        pool.wait_ge(s_added, b * (16 * C) + 16 * (c + 1))
                    pool.sem_inc(s_landed, 1)
            for t in range(T):
                pool.wait_ge(s_dinv[t], nt * (16 * 2 * C) + 16 * 2 * C)

        @block.tensor
        def _(pe):
            pe.wait_ge(pool_const, 11)
            pe.wait_ge(prep_stat, 1)
            pe.transpose(ps_t[0:2, 0, 0:P], n_canon[:], ident[:]).then_inc(prep_pe, 1)
            pe.wait_ge(carry_ready, 1)
            pe.transpose(ps_t[:, 1, 0:1], row2[0:1, 0, :], ident[0:1, 0:1]).then_inc(prep_pe, 1)
            pe.wait_ge(prep_stat, 2)
            pe.matmul(ps_hid[:, 0, 0:1], ones[:], n_canon[:, 1:2], start=True, stop=True).then_inc(prep_pe, 1)
            pe.wait_ge(prep_stat, 3)
            pe.transpose(ps_t[0:1, 0, 0:P], n_extra[:], ident[:]).then_inc(prep_pe, 1)

            for k in range(2):
                pe.matmul(ps_deg[:, k, 0:NHALF], zeros16[:, 0:P], zeros16[:, 0:NHALF], start=True, stop=False)
            nt = load_turns(pe)
            pe.wait_ge(weights_loaded, 16 * 6)

            def turn_half(H, j):
                pe.wait_ge(a_norm, norm_done(H))
                for k in range(2):
                    pe.wait_ge(a_evac, done(H - 1, 2, k))
                    for c in range(HC):
                        mm = pe.transpose(ps_t[:, k, c * P:(c + 1) * P], xn[:, j % E, k * HC + c, :], ident[:])
                    mm.then_inc(a_turned, 1)

            def hidden_half(H, j):
                pe.wait_ge(a_evac, done(H, 2, 1))
                pe.wait_ge(a_gelu, done(H - 2))
                for k in range(2):
                    mm = pe.matmul(ps_hid[0:HID, j % 2, :], w1_sb[:, k, :],
                                   xn[:, j % E, k * HC:(k + 1) * HC, :].rearrange("p c f -> p (c f)"),
                                   start=(k == 0), stop=(k == 1))
                mm.then_inc(a_hid, 1)

            def xt_half(H, j):
                pe.wait_ge(a_msg, done(H - 1))
                for c in range(HC):
                    mm = pe.matmul(ps_xt[:, 0, c * F:(c + 1) * F], xn[:, j % E, c, :], conv_sb[:],
                                   start=True, stop=True)
                mm.then_inc(a_xt, 1)

            def logit_half(H, j):
                pe.wait_ge(a_gelu, done(H))
                pe.wait_ge(a_tanh, done(H - 2))
                for c in range(HC):
                    mm = pe.matmul(ps_z[:, j % 2 * HC + c:j % 2 * HC + c + 1], gel[:, j % 2, c * P:(c + 1) * P],
                                   w2_col[:], start=True, stop=True)
                mm.then_inc(a_z, 1)

            def degree_half(H):
                for c in range(HC):
                    pe.wait_ge(a_hot, H * HC + (c + 1))
                    for part in range(2):
                        for k in range(2):
                            mm = pe.matmul(ps_deg[:, k, 0:NHALF], hot_hi[:, c, part, :],
                                           hot_lo[:, c, k * NHALF:(k + 1) * NHALF], start=False, stop=False)
                    mm.then_inc(a_deg, 1)

            def edge_step(turn, j):
                H = turn * E + j
                turn_half(H, j)
                hidden_half(H, j)
                xt_half(H, j)
                logit_half(H, j)
                if j:
                    degree_half(H - 1)

            edge_steps(pe, nt, edge_step)
            for k in range(2):
                mm = pe.matmul(ps_deg[:, k, 0:NHALF], zeros16[:, 0:P], zeros16[:, 0:NHALF], start=False, stop=True)
            mm.then_inc(deg_all, 1)

            pe.wait_ge(edges_deg, 1)
            xt_banks = (ps_xt[:, 0], ps_deg[:, 1])

            def xt_group(g, s, r, again):
                for k in range(2):
                    if again or g >= 1:
                        pe.wait_ge(n_out, g * 2 + (k - 1))
                    for c in range(HJ):
                        mm = pe.matmul(xt_banks[k][:, c * F:(c + 1) * F], xn[:, s, k * HJ + c, :], conv_sb[:],
                                       start=True, stop=True)
                    mm.then_inc(n_xt, 1)

            def turn_group(g, s, r, again):
                pe.wait_ge(n_norm, g + 1)
                for k in range(2):
                    if again or g >= 1:
                        pe.wait_ge(n_evac, g * 2 + (k - 1))
                    for c in range(HJ):
                        mm = pe.transpose(ps_t[:, k, c * P:(c + 1) * P], xn[:, s, k * HJ + c, :], ident[:])
                    mm.then_inc(n_turned, 1)

            def logit_group(g, s, r, again):
                for k in range(2):
                    pe.wait_ge(n_gelu, g * 2 + (k + 1))
                    for c in range(HJ):
                        at = s * J + k * HJ + c
                        mm = pe.matmul(ps_z[:, at:at + 1], gel[:, k, c * P:(c + 1) * P], w2_col[:],
                                       start=True, stop=True)
                    mm.then_inc(n_z, 1)

            def hidden_group(g, s, r, again):
                for k in range(2):
                    pe.wait_ge(n_evac, g * 2 + (k + 1))
                    if again or g >= 1:
                        pe.wait_ge(n_gelu, g * 2 + (k - 1))
                    pe.matmul(ps_hid[0:HID, k, :], w1_sum[:],
                              xn[:, s, k * HJ:(k + 1) * HJ, :].rearrange("p c f -> p (c f)"),
                              start=True, stop=True).then_inc(n_hid, 1)

            pipeline(pe, [(turn_group, 2), (logit_group, 4), (xt_group, 4), (hidden_group, 3)])

            def merge(b, c):
                pe.wait_ge(s_same, b * C + (c + 1 + 2))
                pe.wait_ge(s_merged, b * C + (c + 1))
                pe.matmul(ps_hid[:, c % 2, 0:F], same[:, c % 2, :], msg_s[:, c, :],
                          start=True, stop=True).then_inc(s_sum, 1)

            with pe.Fori(0, nt) as turn:
                for t in range(T):
                    b = turn * T + t
                    pe.wait_ge(s_dst, b + 1)
                    for c in range(C):
                        pe.wait_ge(s_same, b * C + (c + 1))
                        pe.transpose(ps_t[:, c % 2, 0:P], dcol_f[:, c:c + 1].to_broadcast([P, P]),
                                     ident[:]).then_inc(s_turned, 1)
                        if c == 0:
                            pe.wait_ge(s_msg, b + (T + 1))
                        if c >= 1:
                            merge(b, c - 1)
                    merge(b, C - 1)

        @block.scalar
        def _(act):
            act.wait_ge(weights_loaded, 16 * 6)
            act.activation(gelu_warm[:], b2_all[:], ACT.Gelu)
            act.activation(b2_half[:], b2_all[:], ACT.Copy, scale=0.5).then_inc(n_warm, 1)
            act.wait_ge(n_warm, 1)
            nt = load_turns(act)

            def normalise(s, rows=range(J)):
                for c in rows:
                    last = act.activation(xn[:, s, c, :], xin[:, s, c, :], ACT.Relu, bias=shift[:, s, c:c + 1],
                                          scale=rstd[:, s, c:c + 1])
                return last

            def norm_half(H, j):
                act.wait_ge(a_rstd, done(H))
                act.wait_ge(a_xt, done(H - 2))
                normalise(j % E).then_inc(a_norm, 1)

            def evac_half(H, j):
                for k in range(2):
                    act.wait_ge(a_turned, done(H, 2, k))
                    act.activation(xn[:, j % E, k * HC:(k + 1) * HC, :].rearrange("p c f -> p (c f)"),
                                   ps_t[:, k, :], ACT.Copy).then_inc(a_evac, 1)

            def gelu_half(H, j):
                act.wait_ge(a_hid, done(H))
                act.wait_ge(a_z, done(H - 2))
                act.activation(gel[:, j % 2, :], ps_hid[0:HID, j % 2, :], ACT.Gelu,
                               bias=b1_col[:]).then_inc(a_gelu, 1)

            def tanh_half(H, j):
                act.wait_ge(a_z, done(H))
                act.wait_ge(a_w, done(H - 2))
                act.activation(w_tanh[:, j % 2, :], ps_z[:, j % 2 * HC:(j % 2 + 1) * HC], ACT.Tanh,
                               bias=b2_half[:], scale=0.5).then_inc(a_tanh, 1)

            def message_half(H, j):
                act.wait_ge(a_w, done(H))
                act.wait_ge(a_xt, done(H))
                act.wait_ge(a_xout, done(H - 2))
                for c in range(HC):
                    last = act.activation(xmsg[:, j % 2, c, :], ps_xt[:, 0, c * F:(c + 1) * F], ACT.Copy,
                                          scale=w_col[:, j % 2, c:c + 1])
                last.then_inc(a_msg, 1)

            def edge_step(turn, j):
                H = turn * E + j
                evac_half(H, j)
                if j:
                    message_half(H - 1, j - 1)
                gelu_half(H, j)
                tanh_half(H, j)
                norm_half(H + 1, j + 1)

            norm_half(0, 0)
            edge_steps(act, nt, edge_step)
            act.wait_ge(edges_deg, 1)

            def norm_first(g, s, r, again):
                act.wait_ge(n_rstd, g + 1)
                normalise(s, range(HJ))

            def norm_rest(g, s, r, again):
                normalise(s, range(HJ, J)).then_inc(n_norm, 1)

            def gelu_group(g, s, r, again):
                for k in range(2):
                    act.wait_ge(n_hid, g * 2 + (k + 1))
                    if again or g >= 1:
                        act.wait_ge(n_z, g * 2 + (k - 1))
                    act.activation(gel[:, k, :], ps_hid[0:HID, k, :], ACT.Gelu, bias=b1_col[:]).then_inc(n_gelu, 1)

            def evac_group(g, s, r, again):
                for k in range(2):
                    act.wait_ge(n_turned, g * 2 + (k + 1))
                    act.activation(xn[:, s, k * HJ:(k + 1) * HJ, :].rearrange("p c f -> p (c f)"),
                                   ps_t[:, k, :], ACT.Copy).then_inc(n_evac, 1)

            def tanh_group(g, s, r, again):
                act.wait_ge(n_z, g * 2 + 2)
                act.activation(node_tanh[:, s, :], ps_z[:, s * J:(s + 1) * J], ACT.Tanh, bias=b2_half[:],
                               scale=0.5).then_inc(n_tanh, 1)

            pipeline(act, [(evac_group, 2), (norm_first, 1), (tanh_group, 4), (norm_rest, 1), (gelu_group, 3)])

            act.wait_ge(c_deg, 1)
            act.activation(t_b[:], deg[:], ACT.Sqrt).then_inc(c_sqrt, 1)

            with act.Fori(0, nt) as turn:
                for t in range(T):
                    b = turn * T + t
                    act.wait_ge(s_scale, b + 1)
                    act.wait_ge(s_msg_in, b * 16 + 16)
                    act.wait_ge(s_sum, b * C + 2)
                    for c in range(C):
                        last = act.activation(msg_s[:, c, :], msg[:, c, :], ACT.Copy, scale=scale[:, t, c:c + 1])
                    last.then_inc(s_msg, 1)
                    for c in range(C):
                        act.wait_ge(s_sum, b * C + (c + 3))
                        if c == 0:
                            act.wait_ge(s_landed, b + 1)
                        act.activation(merged[:, t, c, :], ps_hid[:, c % 2, 0:F], ACT.Copy).then_inc(s_merged, 1)

        @block.vector
        def _(dve):
            def chain(semaphore, base=0):
                count = [0]

                def link(ins):
                    count[0] += 1
                    ins.then_inc(semaphore, 1)
                    dve.wait_ge(semaphore, base + count[0])
                return link, count

            link, _ = chain(prep_vec)
            dve.memset(highest[:, 0:1], 0.0)
            for s, n in credits:
                dve.sem_inc(s, n)
            dve.wait_ge(edges_loaded, 32)
            dve.tensor_copy(src_f[:], src_i[:])
            link(dve.tensor_copy(dst_f[:], dst_i[:]))
            link(dve.tensor_tensor(canon[:], src_f[:], dst_f[:], ALU.is_equal))
            link(dve.scalar_tensor_tensor(loop_dst[:], dst_f[:], 1.0, canon[:], ALU.add, ALU.mult))
            link(dve.tensor_tensor_scan(highest[:, 1:], loop_dst[:], loop_dst[:], 0.0, ALU.max, ALU.max))
            dve.tensor_copy(n_canon[:, 1:2], highest[:, EPP:EPP + 1])
            dve.tensor_copy(n_canon[:, 0:1], highest[:, EPP:EPP + 1]).then_inc(prep_stat, 1)
            dve.wait_ge(prep_pe, 1)
            link(dve.tensor_copy(row2[0:1, 1, :], ps_t[0:1, 0, 0:P]))
            dve.memset(row2[0:1, 0, 0:1], 0.0)
            dve.tensor_tensor_scan(row2[0:1, 0, 1:P], row2[0:1, 1, 0:P - 1], row2[0:1, 1, 0:P - 1], 0.0,
                                   ALU.max, ALU.max).then_inc(carry_ready, 1)
            dve.wait_ge(prep_pe, 2)
            link(dve.tensor_copy(carry[:], ps_t[:, 1, 0:1]))
            link(dve.scalar_tensor_tensor(canon[:], highest[:, 0:EPP], carry[:], loop_dst[:], ALU.max, ALU.is_lt))
            dve.reduce_sum(n_canon[:, 1:2], canon[:], AX_X).then_inc(prep_stat, 1)
            dve.wait_ge(prep_pe, 3)
            link(dve.tensor_scalar(all_canon[:], ps_hid[:, 0, 0:1], float(n_nodes + 1), None, ALU.is_equal))
            link(dve.tensor_scalar(half_canon[:], all_canon[:], 0.5, None, ALU.mult))
            dve.tensor_scalar(half_canon1[:], half_canon[:], 1.0, None, ALU.add)
            dve.wait_ge(pool_const, 11)
            link(dve.tensor_scalar(canon[:], canon[:], all_canon[:], 0.0, ALU.mult, ALU.is_equal))
            link(dve.scalar_tensor_tensor(canon[:], dst_f[:], float(PAD), canon[:], ALU.is_lt, ALU.mult))
            link(dve.tensor_copy(extra[:], canon[:]))
            dve.reduce_sum(n_extra[:], canon[:], AX_X).then_inc(prep_stat, 1)
            link(dve.tensor_scalar(pos_key[:], pos_key[:], VALUE_BITS, None, ALU.logical_shift_left))
            for key, node in ((src_key, src_i), (dst_key, dst_i)):
                link(dve.tensor_tensor(full_key[:], pos_key[:], node[:], ALU.bitwise_or))
                link(dve.copy_predicated(key[:, 0:EPP].bitcast(I32), extra[:], full_key[:]))
            dve.wait_ge(prep_pe, 4)
            link(dve.reduce_max(most[:, 0:1], ps_t[0:1, 0, 0:P], AX_X))
            link(dve.tensor_scalar(n_turns_i[:, 1:2], most[:, 0:1], float(T * C - 1), float(T * C), ALU.add, ALU.max))
            dve.tensor_scalar(n_turns_i[:, 0:1], n_turns_i[:, 1:2], (T * C).bit_length() - 1, None,
                              ALU.logical_shift_right).then_inc(turns_known, 1)
            dve.tensor_copy(hi_iota[:], hi_iota_i[:])
            dve.tensor_copy(lo_iota[:], lo_iota_i[:])
            dve.tensor_copy(trash[:], trash_i[:])
            dve.wait_ge(weights_loaded, 16 * 6)
            link(dve.tensor_tensor(w1_sum[:], w1_sb[:, 0, :], w1_sb[:, 1, :], ALU.add))

            nt = load_turns(dve)

            SORT_LINKS = 7
            mask = (1 << VALUE_BITS) - 1

            def sort_src(b):
                link, n = chain(sort_vec, b * SORT_LINKS)
                link(dve.max(best[:, 0, :], src_key[:]))
                dve.tensor_scalar(src_col[:, bass.ds(b * C, C)], best[:, 0, :].bitcast(I32), mask, None,
                                  ALU.bitwise_and)
                dve.match_replace(src_key[:], best[:, 0, :], src_key[:], pad_float)
                assert n[0] == 1, n[0]

            def sort_dst(b):
                link, n = chain(sort_vec, b * SORT_LINKS + 1)
                cols = bass.ds(b * C, C)
                link(dve.max(best[:, 1, :], dst_key[:]))
                dve.tensor_scalar(dst_col[:, cols], best[:, 1, :].bitcast(I32), mask, None,
                                  ALU.bitwise_and).then_inc(sorted_block, 1)
                dve.wait_ge(sorted_block, b + 1)
                dve.tensor_scalar(d_f[:], dst_col[:, cols], 0.0, None, ALU.add)
                link(dve.match_replace(dst_key[:], best[:, 1, :], dst_key[:], pad_float))
                link(dve.tensor_scalar(d_q[:], d_f[:], 1.0 / NPP, 0.5 / NPP - 0.5, ALU.mult, ALU.add))
                link(dve.tensor_scalar(d_r[:], d_q[:], ROUND, None, ALU.add))
                link(dve.tensor_scalar(d_q[:], d_r[:], ROUND, None, ALU.subtract))
                dve.tensor_copy(hi_col[:, cols], d_q[:])
                link(dve.scalar_tensor_tensor(lo_col[:, cols], d_q[:], -float(NPP), d_f[:], ALU.mult, ALU.add))
                assert n[0] == SORT_LINKS - 1, n[0]

            MOMENT_LINKS = 4

            def moments(s, link):
                for c in range(J):
                    last = dve.bn_stats(stats[:, s, c, :], xin[:, s, c, :])
                link(last)
                dve.tensor_tensor(m_sum[:, s, :], stats[:, s, :, 1], stats[:, s, :, 4], ALU.add)
                dve.tensor_tensor(m2[:, s, :], stats[:, s, :, 2], stats[:, s, :, 5], ALU.add)
                link(dve.tensor_tensor(m_dif[:, s, :], stats[:, s, :, 1], stats[:, s, :, 4], ALU.subtract))
                dve.tensor_scalar(neg_mean[:, s, :], m_sum[:, s, :], -0.5, None, ALU.mult)
                link(dve.tensor_tensor(m_dif[:, s, :], m_dif[:, s, :], m_dif[:, s, :], ALU.mult))
                link(dve.scalar_tensor_tensor(m2[:, s, :], m_dif[:, s, :], F / 4.0, m2[:, s, :], ALU.mult, ALU.add))
                return dve.tensor_scalar(var[:, s, :], m2[:, s, :], 1.0 / F, EPS, ALU.mult, ALU.add)

            LN_LINKS = MOMENT_LINKS + 12

            def one_hot(H, c, k):
                if k == 0:
                    dve.wait_ge(a_deg, done(H - 1, HC, c))
                at = H * HC + c
                if k < 2:
                    dve.tensor_scalar(hot_hi[:, c, k, :], hi_iota[:], hi_col[:, bass.ds(at, 1)],
                                      w_part[:, k, c:c + 1], ALU.is_equal, ALU.mult)
                else:
                    dve.tensor_scalar(hot_lo[:, c, :], lo_iota[:], lo_col[:, bass.ds(at, 1)], None,
                                      ALU.is_equal).then_inc(a_hot, 1)

            def ln_half(turn, j, with_hot):
                H = turn * E + j
                slot = j % E
                count = [0]

                def link(ins, c=None, k=None):
                    count[0] += 1
                    ins.then_inc(a_ln, 1)
                    if with_hot and c is not None:
                        one_hot(H - 2, c, k)
                    dve.wait_ge(a_ln, H * LN_LINKS + count[0])

                dve.wait_ge(gathered[slot], turn * (16 * 2 * HC) + 16 * 2 * HC * (j // E + 1))
                link(moments(slot, link), 0, 0)
                y, v, t = rstd[:, slot, :], var[:, slot, :], m_dif[:, slot, :]
                link(dve.tensor_scalar(y.bitcast(I32), v.bitcast(I32), 1, None, ALU.logical_shift_right), 0, 1)
                dve.tensor_scalar(v, v, -0.5, None, ALU.mult)
                link(dve.tensor_scalar(y.bitcast(I32), y.bitcast(I32), -1.0, float(0x5F3759DF), ALU.mult, ALU.add),
                     0, 2)
                for c in range(1, HC):
                    link(dve.tensor_tensor(t, y, y, ALU.mult), c, 0)
                    link(dve.tensor_tensor(t, t, v, ALU.mult), c, 1)
                    link(dve.scalar_tensor_tensor(y, t, 1.5, y, ALU.add, ALU.mult), c, 2)
                dve.tensor_tensor(shift[:, slot, :], neg_mean[:, slot, :], y, ALU.mult).then_inc(a_rstd, 1)
                assert count[0] == LN_LINKS, count[0]

            def weight_half(H, j):
                link, n = chain(a_post, H * 2)
                h = j % 2
                dve.wait_ge(a_tanh, done(H))
                dve.wait_ge(a_msg, done(H - 2))
                dve.tensor_scalar(w_col[:, h, :], w_tanh[:, h, :], 0.5, 0.5, ALU.mult, ALU.add)
                dve.tensor_scalar(w_part[:, 0, :], w_tanh[:, h, :], W_SCALE / 2, W_SCALE / 2, ALU.mult,
                                  ALU.add).then_inc(a_w, 1)
                dve.wait_ge(a_w, done(H))
                link(dve.tensor_copy(w_16[:], w_part[:, 0, :]))
                link(dve.tensor_tensor(w_part[:, 1, :], w_part[:, 0, :], w_16[:], ALU.subtract))
                assert n[0] == 2

            def edge_step(turn, j):
                if j:
                    weight_half(turn * E + (j - 1), j - 1)
                ln_half(turn, j + 1, j > 0)
                b = turn * T + (j // 2 + 2)
                if j % 2:
                    sort_dst(b)
                else:
                    sort_src(b)

            sort_src(0)
            sort_dst(0)
            sort_src(1)
            sort_dst(1)
            ln_half(0, 0, False)
            edge_steps(dve, nt, edge_step)
            dve.wait_ge(deg_all, 1)
            dve.wait_ge(a_norm, nt * E + (E + 2))
            for k in range(2):
                last = dve.tensor_scalar(deg[:, k * NHALF:(k + 1) * NHALF], ps_deg[:, k, 0:NHALF], 1.0 / W_SCALE,
                                         None, ALU.mult)
            last.then_inc(edges_deg, 1)
            dve.wait_ge(edges_deg, 1)
            for h in range(2):
                dve.wait_ge(a_stored[h], nt * (16 * E // 2))

            NODE_LINKS = MOMENT_LINKS

            def node_moments(g, s, r, again):
                link, n = chain(n_vec, g * NODE_LINKS)
                dve.wait_ge(n_loaded[s], r * 16 + 16)
                moments(s, link).then_inc(n_var, 1)
                assert n[0] == NODE_LINKS, n[0]

            COEF_LINKS = 4

            def node_coef(g, s, r, again):
                link, n = chain(n_coef, g * COEF_LINKS)
                cols = bass.ds(g * J, J)
                dve.wait_ge(n_tanh, g + 1)
                link(dve.tensor_scalar(self_w[:, s, :], node_tanh[:, s, :], half_canon[:], half_canon1[:],
                                       ALU.mult, ALU.add))
                link(dve.tensor_tensor(deg[:, cols], deg[:, cols], self_w[:, s, :], ALU.add))
                dve.scalar_tensor_tensor(self_w[:, s, :], deg[:, cols], 0.0, self_w[:, s, :],
                                         ALU.is_gt, ALU.mult)
                link(dve.reciprocal(deg_rec[:, s, :], deg[:, cols]))
                link(dve.tensor_tensor(coef[:, s, :], self_w[:, s, :], deg_rec[:, s, :], ALU.mult))
                assert n[0] == COEF_LINKS, n[0]

            def node_out(g, s, r, again):
                dve.wait_ge(n_bias, g + 1)
                for k in range(2):
                    dve.wait_ge(n_xt, g * 2 + (k + 1))
                    bank = (ps_xt[:, 0], ps_deg[:, 1])[k]
                    for c in range(HJ):
                        t = k * HJ + c
                        last = dve.scalar_tensor_tensor(xin[:, s, t, :], bank[:, c * F:(c + 1) * F],
                                                        coef[:, s, t:t + 1], xin[:, s, t, :], ALU.mult, ALU.add)
                    last.then_inc(n_out, 1)

            pipeline(dve, [(node_moments, 0), (node_coef, 4), (node_out, 4)])

            link, _ = chain(c_vec)
            dve.sem_inc(c_deg, 1)
            dve.wait_ge(c_sqrt, 1)
            link(dve.reciprocal(dinv[:], t_b[:]))
            link(dve.tensor_tensor(t_b[:], dinv[:], dinv[:], ALU.mult))
            link(dve.tensor_tensor(t_b[:], t_b[:], deg[:], ALU.mult))
            link(dve.tensor_scalar(t_b[:], t_b[:], -0.5, 1.5, ALU.mult, ALU.add))
            link(dve.tensor_tensor(dinv[:], dinv[:], t_b[:], ALU.mult))
            dve.scalar_tensor_tensor(dinv[:], deg[:], 0.0, dinv[:], ALU.is_gt, ALU.mult).then_inc(c_dinv, 1)

            S_LINKS = 3
            with dve.Fori(0, nt) as turn:
                for t in range(T):
                    b = turn * T + t
                    link, n = chain(s_vec, b * S_LINKS)
                    dve.wait_ge(s_turned, b * C + 1)
                    dve.wait_ge(s_row, b + 1)
                    dve.tensor_copy(dcol_f[:], dst_col[:, bass.ds(b * C, C)]).then_inc(s_dst, 1)
                    dve.wait_ge(s_dinv[t], turn * (16 * 2 * C) + 16 * 2 * C)
                    dve.wait_ge(s_msg, b + 1)
                    dve.tensor_tensor(scale[:, t, :], dinv_g[:, t, 0, :], dinv_g[:, t, 1, :], ALU.mult).then_inc(s_scale, 1)
                    for c in range(C):
                        dve.wait_ge(s_turned, b * C + (c + 2))
                        dve.wait_ge(s_sum, b * C + (c + 1))
                        dve.tensor_scalar(same[:, c % 2, :], ps_t[:, c % 2, 0:P], dcol_f[:, c:c + 1], None,
                                          ALU.is_equal).then_inc(s_same, 1)
                        dve.wait_ge(s_same, b * C + (c + 3))
                        last = dve.tensor_tensor_reduce(same_low[:], same[:, c % 2, :], lower[:], 1.0, 0.0, ALU.mult,
                                                        ALU.add, prior[:, c:c + 1])
                    link(last)
                    link(dve.tensor_scalar(to_trash[:], dcol_f[:], -1.0, trash[:], ALU.mult, ALU.add))
                    link(dve.scalar_tensor_tensor(row_f[:], prior[:], 0.0, to_trash[:], ALU.is_gt, ALU.mult))
                    dve.tensor_tensor(row_col[:, bass.ds(b * C, C)], row_f[:], dcol_f[:], ALU.add).then_inc(s_row, 1)
                    assert n[0] == S_LINKS


def kernel(x, src, dst, L0_gnn_mlp_w1, L0_gnn_mlp_b1, L0_gnn_mlp_w2, L0_gnn_mlp_b2, L0_gnn_conv_w, L0_gnn_conv_b):
    import numpy as np
    import concourse.bacc as bacc
    from concourse.bass_utils import run_bass_kernel_spmd

    x = np.asarray(x)
    n_nodes, n_edges = x.shape[0], np.asarray(src).shape[0]
    npp, epp = sizes(n_nodes, n_edges)
    arrays = {
        "x": np.zeros((P * npp, F), np.float32),
        "src": np.full(P * epp, n_nodes, np.int32),
        "dst": np.full(P * epp, n_nodes, np.int32),
    }
    arrays["x"][:n_nodes] = x
    arrays["src"][:n_edges] = np.asarray(src)
    arrays["dst"][:n_edges] = np.asarray(dst)
    arrays["src"] = arrays["src"].reshape(P, epp)
    arrays["dst"] = arrays["dst"].reshape(P, epp)
    arrays["w1"] = np.ascontiguousarray(L0_gnn_mlp_w1)
    arrays["b1"] = np.asarray(L0_gnn_mlp_b1).reshape(HID, 1)
    arrays["w2"] = np.asarray(L0_gnn_mlp_w2).reshape(HID, 1)
    arrays["b2"] = np.asarray(L0_gnn_mlp_b2).reshape(1, 1)
    arrays["conv_w"] = np.ascontiguousarray(L0_gnn_conv_w)
    arrays["conv_b"] = np.asarray(L0_gnn_conv_b).reshape(1, F)

    nc = bacc.Bacc("TRN2", target_bir_lowering=False, num_devices=1)
    aps = [nc.dram_tensor(f"in_{n}", a.shape, mybir.dt.from_np(a.dtype), kind="ExternalInput").ap()
           for n, a in arrays.items()]
    out = nc.dram_tensor("out", (P * npp, F), F32, kind="ExternalOutput").ap()
    gnn_layer(nc, n_nodes, *aps, out)
    r = run_bass_kernel_spmd(nc, [{f"in_{n}": a for n, a in arrays.items()}], core_ids=[0])
    return r.results[0]["out"][:n_nodes]
```

```python
from contextlib import ExitStack

import concourse.bass as bass
from concourse import mybir

P = 128
C = 8
HC = C // 2
T = 2
E = 4
LEAD = 3
Q = C // 2
J = 8
HJ = J // 2
R = 7
F = 128
HID = 64
BANK = 512
VALUE_BITS = 17
KEY_BASE = 1 << 29
W_SCALE = 4096.0
ROUND = 1.5 * (1 << 23)
EPS = 1e-5

ALU = mybir.AluOpType
ACT = mybir.ActivationFunctionType
AX_X = mybir.AxisListType.X
F32 = mybir.dt.float32
F16 = mybir.dt.float16
I32 = mybir.dt.int32
U32 = mybir.dt.uint32


def sizes(n_nodes, n_edges):
    npp = -(-(n_nodes + 2 * P + 1) // P)
    npp = -(-npp // (R * J)) * R * J
    epp = -(-(n_edges + 1) // P)
    return npp, epp


def node_index(ap, npp):
    return ap.rearrange("(p j) f -> p j f", j=npp)


def gnn_layer(nc, n_nodes, x, src, dst, w1, b1, w2, b2, conv_w, conv_b, out):
    NP = x.shape[0]
    NPP = NP // P
    NHALF = NPP // 2
    G = NPP // J
    EPP = src.shape[1]
    NT_MAX = max(-(-EPP // (T * C)), 2)
    EW = NT_MAX * T * C
    CW = EW + (LEAD + 1) * C
    PAD = n_nodes
    PAD_KEY = KEY_BASE | PAD
    assert NP < 1 << VALUE_BITS and NHALF <= BANK and NP >= n_nodes + 2 * P + 1
    assert EPP + 1 < 1 << (29 - VALUE_BITS)

    import numpy as np
    pad_float = float(np.array([PAD_KEY], np.int32).view(np.float32)[0])

    msg_dram = nc.dram_tensor("msg_dram", [P, CW * F], F32, kind="Internal").ap()
    dinv_dram = nc.dram_tensor("dinv_dram", [NP, 1], F32, kind="Internal").ap()

    x_t = node_index(x, NPP)
    out_t = node_index(out, NPP)

    with ExitStack() as ctx:
        def sb(name, shape, dt=F32):
            return ctx.enter_context(nc.sbuf_tensor(name, shape, dt))

        def sem(name):
            return ctx.enter_context(nc.semaphore(name))

        ps_t = ctx.enter_context(nc.psum_tensor("ps_t", [P, 2, BANK], F32))
        ps_hid = ctx.enter_context(nc.psum_tensor("ps_hid", [P, 2, BANK], F32))
        ps_xt = ctx.enter_context(nc.psum_tensor("ps_xt", [P, 2, BANK], F32))
        ps_deg = ctx.enter_context(nc.psum_tensor("ps_deg", [P, 2, BANK], F32))

        table_banks = (ps_deg, ps_hid)
        ps_z = ps_xt[:, 1]

        ident = sb("ident", [P, P])
        ones = sb("ones", [P, P])
        lower = sb("lower", [P, 2 * P])
        trash = sb("trash", [P, C])
        trash_i = sb("trash_i", [P, Q, 2], I32)
        part_i = sb("part_i", [P, 1], I32)
        part = sb("part", [P, 1])
        hi_iota_i = sb("hi_iota_i", [P, P], I32)
        hi_iota = sb("hi_iota", [P, P], F16)
        lo_iota_i = sb("lo_iota_i", [P, NPP], I32)
        lo_iota = sb("lo_iota", [P, NPP], F16)
        zeros16 = sb("zeros16", [P, BANK], F16)
        w1_sb = sb("w1_sb", [P, 2, HID])
        w1_sum = sb("w1_sum", [P, HID])
        conv_sb = sb("conv_sb", [P, F])
        b1_col = sb("b1_col", [2 * HID, 1])
        w2_pair = sb("w2_pair", [2 * HID, 2])
        b2_all = sb("b2_all", [P, 1])
        b2_half = sb("b2_half", [P, 1])
        cb_all = sb("cb_all", [P, F])
        half_canon = sb("half_canon", [P, 1])
        half_canon1 = sb("half_canon1", [P, 1])
        gelu_warm = sb("gelu_warm", [P, 1])
        pow_exp = sb("pow_exp", [P, J])

        src_i = sb("src_i", [P, EPP], I32)
        dst_i = sb("dst_i", [P, EPP], I32)
        src_f = sb("src_f", [P, EPP])
        dst_f = sb("dst_f", [P, EPP])
        loop_dst = sb("loop_dst", [P, EPP])
        highest = sb("highest", [P, EPP + 1])
        canon = sb("canon", [P, EPP])
        n_canon = sb("n_canon", [P, 2])
        row2 = sb("row2", [1, 2, P])
        carry = sb("carry", [P, 1])
        all_canon = sb("all_canon", [P, 1])
        extra = sb("extra", [P, EPP], U32)
        n_extra = sb("n_extra", [P, 1])
        most = sb("most", [1, 2])
        n_turns_i = sb("n_turns_i", [1, 2], I32)
        pos_key = sb("pos_key", [P, EPP], I32)
        full_key = sb("full_key", [P, EPP], I32)
        src_key = sb("src_key", [P, EW])
        dst_key = sb("dst_key", [P, EW])
        best = sb("best", [P, 2, C])
        src_col = sb("src_col", [P, CW], I32)
        dst_col = sb("dst_col", [P, CW], I32)
        gather_idx = sb("gather_idx", [P, E, 2 * HC], I32)

        xin = sb("xin", [P, R, J, F])
        xn = sb("xn", [P, R, J, F])
        gel = sb("gel", [HID, 2, BANK])
        node_gel = sb("node_gel", [2 * HID, BANK])
        xmsg = sb("xmsg", [P, 2, HC, F])
        stats = sb("stats", [P, R, J, 6])
        m_sum = sb("m_sum", [P, R, J])
        m_dif = sb("m_dif", [P, R, J])
        m2 = sb("m2", [P, R, J])
        neg_mean = sb("neg_mean", [P, R, J])
        var = sb("var", [P, R, J])
        rstd = sb("rstd", [P, R, J])
        shift = sb("shift", [P, R, J])
        w_tanh = sb("w_tanh", [P, 2, HC])
        w_col = sb("w_col", [P, 2, HC])
        w_16 = sb("w_16", [P, HC], F16)
        w_scaled = sb("w_scaled", [P, HC])
        w_part = sb("w_part", [P, 2, 2, HC])
        d_f = sb("d_f", [P, C])
        d_q = sb("d_q", [P, C])
        d_r = sb("d_r", [P, C])
        hi_col = sb("hi_col", [P, CW])
        lo_col = sb("lo_col", [P, CW])
        hot_mask = sb("hot_mask", [P, 2, HC, P], F16)
        hot_hi = sb("hot_hi", [P, HC, 2, P], F16)
        hot_lo = sb("hot_lo", [P, 2, HC, NPP], F16)

        node_tanh = sb("node_tanh", [P, R, J])
        self_w = sb("self_w", [P, R, J])
        deg_rec = sb("deg_rec", [P, NPP])
        coef = sb("coef", [P, R, J])
        deg = sb("deg", [P, NPP])
        dinv = sb("dinv", [P, NPP])
        t_b = sb("t_b", [P, NPP])
        dinv_16 = sb("dinv_16", [P, 2, NPP], F16)

        dinv_idx = sb("dinv_idx", [P, T, C], I32)
        dinv_src = sb("dinv_src", [P, T, C])
        dinv_dst = sb("dinv_dst", [P, T, C])
        dcol = sb("dcol", [P, T, C])
        hcol = sb("hcol", [P, T, C])
        lcol = sb("lcol", [P, T, C])
        hot_t = sb("hot_t", [P, 4, P], F16)
        picked = sb("picked", [P, 2, 2, NHALF])
        same = sb("same", [P, 2, 3, P])
        same_a = sb("same_a", [P, P])
        same_b = sb("same_b", [P, 2 * P])
        prior = sb("prior", [P, C])
        to_trash = sb("to_trash", [P, C])
        row_f = sb("row_f", [P, C])
        row_idx = sb("row_idx", [P, T, C], I32)
        msg = sb("msg", [P, C, F])
        msg_s = sb("msg_s", [P, T, C, F])
        merged = xn[:, 0:T]

        edges_loaded = sem("edges_loaded")
        weights_loaded = sem("weights_loaded")
        pool_const = sem("pool_const")
        prep_vec = sem("prep_vec")
        prep_stat = sem("prep_stat")
        prep_pe = sem("prep_pe")
        carry_ready = sem("carry_ready")
        turns_known = sem("turns_known")

        sorted_block = sem("sorted_block")
        sort_vec = sem("sort_vec")
        idx_copied = sem("idx_copied")
        waited = sem("waited")
        gathered = [sem(f"gathered{h}") for h in range(E)]
        a_ln = sem("a_ln")
        a_rstd = sem("a_rstd")
        a_norm = sem("a_norm")
        a_turned = sem("a_turned")
        a_evac = sem("a_evac")
        a_hid = sem("a_hid")
        a_gelu = sem("a_gelu")
        a_z = sem("a_z")
        a_tanh = sem("a_tanh")
        a_w = sem("a_w")
        a_xt = sem("a_xt")
        a_msg = sem("a_msg")
        a_stored = [sem(f"a_stored{h}") for h in range(2)]
        a_hot = sem("a_hot")
        a_rounded = sem("a_rounded")
        a_part = sem("a_part")
        a_scaled = sem("a_scaled")
        a_deg = sem("a_deg")
        a_xout = sem("a_xout")
        deg_all = sem("deg_all")
        edges_deg = sem("edges_deg")

        n_loaded = [sem(f"n_loaded{s}") for s in range(R)]
        n_vec = sem("n_vec")
        n_warm = sem("n_warm")
        n_var = sem("n_var")
        n_pow = sem("n_pow")
        n_rstd = sem("n_rstd")
        n_norm = sem("n_norm")
        n_bias = sem("n_bias")
        n_turned = sem("n_turned")
        n_evac = sem("n_evac")
        n_hid = sem("n_hid")
        n_gelu = sem("n_gelu")
        n_z = sem("n_z")
        n_tanh = sem("n_tanh")
        n_xt = sem("n_xt")
        n_coef = sem("n_coef")
        n_out = sem("n_out")
        n_stored = [sem(f"n_stored{s}") for s in range(R)]

        c_vec = sem("c_vec")
        c_deg = sem("c_deg")
        c_sqrt = sem("c_sqrt")
        c_dinv = sem("c_dinv")
        dinv_stored = sem("dinv_stored")

        s_idx = sem("s_idx")
        s_dinv = [sem(f"s_dinv{t}") for t in range(T)]
        s_dst = sem("s_dst")
        s_turned = sem("s_turned")
        s_hot = sem("s_hot")
        s_table = sem("s_table")
        s_same = sem("s_same")
        s_picked = sem("s_picked")
        s_vec = sem("s_vec")
        s_row = sem("s_row")
        s_msg_in = sem("s_msg_in")
        s_msg = sem("s_msg")
        s_sum = sem("s_sum")
        s_merged = sem("s_merged")
        s_added = sem("s_added")
        s_landed = sem("s_landed")

        block = ctx.enter_context(nc.Block())

        def load_turns(eng):
            eng.wait_ge(turns_known, 1)
            before_last = eng.value_load(n_turns_i[0:1, 0:1], min_val=1, max_val=NT_MAX - 1)
            return before_last, before_last + 1

        def pipeline(eng, stages):
            last = max(lag for _, *lags in stages for lag in lags)
            lead = -(-(last + R) // R) * R
            assert G > lead

            def step(turn, u, at=None):
                for f, *lags in stages:
                    groups = [None if at is not None and not 0 <= at - lag < G else
                              (turn * R + (u - lag), (u - lag) % R, turn + (u - lag) // R,
                               at is None or at - lag >= R) for lag in lags]
                    if len(groups) == 2:
                        f(*groups)
                    elif groups[0] is not None:
                        f(*groups[0])

            for s in range(lead):
                step(s // R, s % R, s)
            with eng.Fori(lead // R, G // R) as turn:
                for u in range(R):
                    step(turn, u)
            for s in range(G, G + last):
                step(s // R, s % R, s)

        credits = ((a_norm, E), (a_rstd, 2), (a_turned, 4), (a_evac, 4), (a_hid, 2), (a_gelu, 2), (a_z, 2),
                   (a_tanh, 2), (a_w, 2), (a_xt, 2), (a_msg, 2), (a_xout, 2), (a_deg, C),
                   (s_landed, T), (s_msg, 1), (s_same, 2), (s_picked, 2), (s_merged, 4), (s_sum, 4))

        def edge_slot(j):
            return R - E + j % E

        def done(half, n=1, i=0):
            return half * n + (2 * n + i + 1)

        def norm_done(half):
            return half + (E + 1)

        def edge_steps(eng, before_last, step):
            step(0, 0, E)
            with eng.Fori(0, before_last) as turn:
                for j in range(1, E + 1):
                    step(turn, j, E)
            for j in range(1, E + 1):
                step(before_last, j, E - 1 - j)

        @block.sync
        def _(sp):
            sp.dma_start(src_i[:], src).then_inc(edges_loaded, 16)
            sp.dma_start(dst_i[:], dst).then_inc(edges_loaded, 16)
            sp.dma_start(w1_sb[:], w1.rearrange("(t p) h -> p t h", p=P)).then_inc(weights_loaded, 16)
            sp.dma_start(conv_sb[:], conv_w).then_inc(weights_loaded, 16)
            sp.wait_ge(pool_const, 1)
            for k in range(2):
                half = slice(k * HID, (k + 1) * HID)
                sp.dma_start(b1_col[half, :], b1).then_inc(weights_loaded, 16)
                sp.dma_start(w2_pair[half, k:k + 1], w2).then_inc(weights_loaded, 16)
            sp.dma_start(b2_all[:], b2.to_broadcast([P, 1])).then_inc(weights_loaded, 16)
            sp.dma_start(cb_all[:], conv_b.to_broadcast([P, F])).then_inc(weights_loaded, 16)

            for g in range(R - E):
                sp.dma_start(xin[:, g], x_t[:, g * J:(g + 1) * J, :]).then_inc(n_loaded[g], 16)

            before_last, nt = load_turns(sp)
            with sp.Fori(0, nt) as turn:
                for j in range(E):
                    H = turn * E + j
                    sp.wait_ge(a_msg, done(H))
                    sp.dma_start(msg_dram[:, bass.ds(H * (HC * F), HC * F)],
                                 xmsg[:, j % 2, :, :].rearrange("p c f -> p (c f)")).then_inc(a_stored[j % 2], 16)
                    sp.wait_ge(a_stored[j % 2], turn * (16 * E // 2) + 16 * (j // 2 + 1))
                    sp.sem_inc(a_xout, 1)
            sp.dma_start(msg_dram[:, bass.ds(nt * (E * HC * F), C * F)],
                         xmsg[:].rearrange("p h c f -> p (h c f)")).then_inc(a_stored[0], 16)

            def load_x(g, s, r, again):
                if not again and g < R - E:
                    return
                if not again and g == R - E:
                    sp.wait_ge(a_norm, norm_done(before_last * E + (E - 1)))
                if again:
                    sp.wait_ge(n_stored[s], r * 16)
                sp.dma_start(xin[:, s], x_t[:, bass.ds(g * J, J), :]).then_inc(n_loaded[s], 16)

            def store_out(g, s, r, again):
                sp.wait_ge(n_out, g * 2 + 2)
                sp.dma_start(out_t[:, bass.ds(g * J, J), :], xin[:, s]).then_inc(n_stored[s], 16)

            pipeline(sp, [(load_x, 0), (store_out, R - 1)])

            sp.wait_ge(c_dinv, 1)
            sp.dma_start(dinv_dram.rearrange("(p j) o -> p (j o)", j=NPP), dinv[:]).then_inc(dinv_stored, 16)

            sp.wait_ge(a_stored[0], nt * (16 * E // 2) + 16)
            sp.dma_start(msg[:].rearrange("p c f -> p (c f)"), msg_dram[:, 0:C * F]).then_inc(s_msg_in, 16)
            with sp.Fori(0, nt) as turn:
                for t in range(T):
                    b = turn * T + t
                    sp.wait_ge(s_msg, b + 2)
                    sp.dma_start(msg[:].rearrange("p c f -> p (c f)"),
                                 msg_dram[:, bass.ds(b * (C * F) + C * F, C * F)]).then_inc(s_msg_in, 16)

        @block.gpsimd
        def _(pool):
            pool.memset(w2_pair[:], 0.0).then_inc(pool_const, 1)
            pool.memset(ones[:], 1.0).then_inc(pool_const, 1)
            pool.wait_ge(pool_const, 2)
            pool.affine_select(out=ident[:], in_=ones[:], compare_op=ALU.is_equal, fill=0.0, base=0,
                               pattern=[[-1, P]], channel_multiplier=1).then_inc(pool_const, 1)
            pool.affine_select(out=lower[:, 0:P], in_=ones[:], compare_op=ALU.is_gt, fill=0.0, base=0,
                               pattern=[[-1, P]], channel_multiplier=1).then_inc(pool_const, 1)
            pool.iota(trash_i[:], pattern=[[0, Q], [P, 2]], base=n_nodes + 1, channel_multiplier=1).then_inc(pool_const, 1)
            pool.iota(hi_iota_i[:], pattern=[[1, P]], base=0, channel_multiplier=0).then_inc(pool_const, 1)
            pool.iota(lo_iota_i[:], pattern=[[1, NPP]], base=0, channel_multiplier=0).then_inc(pool_const, 1)
            pool.iota(pos_key[:], pattern=[[-1, EPP]], base=(KEY_BASE >> VALUE_BITS) + EPP,
                      channel_multiplier=0).then_inc(pool_const, 1)
            pool.memset(zeros16[:], 0.0).then_inc(pool_const, 1)
            pool.memset(lower[:, P:2 * P], 1.0).then_inc(pool_const, 1)
            pool.iota(part_i[:], pattern=[[0, 1]], base=0, channel_multiplier=1).then_inc(pool_const, 1)
            pool.memset(pow_exp[:], -0.5).then_inc(pool_const, 1)
            pool.memset(src_key[:].bitcast(I32), PAD_KEY).then_inc(pool_const, 1)
            pool.memset(dst_key[:].bitcast(I32), PAD_KEY).then_inc(pool_const, 1)

            before_last, nt = load_turns(pool)

            def held():
                pool.sem_inc(waited, 1)

            def gather_half(turn, j):
                H = turn * E + j
                slot = j % E
                pool.wait_ge(sorted_block, turn * T + (j // 2 + 1))
                pool.wait_ge(a_norm, norm_done(H - E))
                pool.tensor_copy(gather_idx[:, slot, 0:HC], src_col[:, bass.ds(H * HC, HC)]).then_inc(idx_copied, 1)
                pool.tensor_copy(gather_idx[:, slot, HC:], dst_col[:, bass.ds(H * HC, HC)]).then_inc(idx_copied, 1)
                pool.wait_ge(idx_copied, H * 2 + 2)
                held()
                for c in range(2 * HC):
                    pool.indirect_dma_start(xin[:, edge_slot(j), c, :], None, x, bass.IndirectOffsetOnAxis(
                        ap=gather_idx[:, slot, c:c + 1], axis=0)).then_inc(gathered[slot], 16)

            gather_half(0, 0)
            gather_half(0, 1)
            with pool.Fori(0, before_last) as turn:
                for j in range(2, E + 2):
                    gather_half(turn, j)
            for j in range(2, E):
                gather_half(before_last, j)

            def add_bias(g, s, r, again):
                pool.wait_ge(n_norm, g + 1)
                pool.tensor_tensor(xin[:, s], xin[:, s], cb_all[:].unsqueeze(1).to_broadcast([P, J, F]),
                                   ALU.add).then_inc(n_bias, 1)

            def power(g, s, r, again):
                pool.wait_ge(n_var, g + 1)
                pool.tensor_tensor(rstd[:, s, :], var[:, s, :], pow_exp[:], ALU.pow).then_inc(n_pow, 1)
                pool.wait_ge(n_pow, g + 1)
                pool.tensor_tensor(shift[:, s, :], neg_mean[:, s, :], rstd[:, s, :], ALU.mult).then_inc(n_rstd, 1)

            pipeline(pool, [(add_bias, 3), (power, 0)])

            def dinv_gather(t, c):
                pool.indirect_dma_start(dinv_src[:, t, c:c + 1], None, dinv_dram, bass.IndirectOffsetOnAxis(
                    ap=dinv_idx[:, t, c:c + 1], axis=0)).then_inc(s_dinv[t], 16)

            pool.wait_ge(dinv_stored, 16)
            for t in range(T):
                pool.wait_ge(s_idx, t + 1)
                for c in range(C):
                    dinv_gather(t, c)
            for s in range(R):
                pool.wait_ge(n_stored[s], 16 * (G // R))
            with pool.Fori(0, nt) as turn:
                for t in range(T):
                    b = turn * T + t
                    for c in range(0, C, 2):
                        if c == 0:
                            pool.wait_ge(s_row, b + 1)
                            pool.wait_ge(s_idx, b + (T + 1))
                        pool.wait_ge(s_merged, b * C + (c + 2 + 4))
                        held()
                        for k in (c, c + 1):
                            pool.indirect_dma_start(out, bass.IndirectOffsetOnAxis(ap=row_idx[:, t, k:k + 1], axis=0),
                                                    merged[:, t, k, :], None, compute_op=ALU.add).then_inc(s_added, 16)
                        for k in (c, c + 1):
                            dinv_gather(t, k)
                        pool.wait_ge(s_added, b * (16 * C) + 16 * (c + 2))
                    pool.sem_inc(s_landed, 1)
            for t in range(T):
                pool.wait_ge(s_dinv[t], nt * (16 * C) + 16 * C)

        @block.tensor
        def _(pe):
            pe.wait_ge(pool_const, 14)
            pe.wait_ge(prep_stat, 1)
            pe.transpose(ps_t[0:2, 0, 0:P], n_canon[:], ident[:]).then_inc(prep_pe, 1)
            pe.wait_ge(carry_ready, 1)
            pe.transpose(ps_t[:, 1, 0:1], row2[0:1, 0, :], ident[0:1, 0:1]).then_inc(prep_pe, 1)
            pe.wait_ge(prep_stat, 2)
            pe.matmul(ps_hid[:, 0, 0:1], ones[:], n_canon[:, 1:2], start=True, stop=True).then_inc(prep_pe, 1)
            pe.wait_ge(prep_stat, 3)
            pe.transpose(ps_t[0:1, 0, 0:P], n_extra[:], ident[:]).then_inc(prep_pe, 1)

            for k in range(2):
                pe.matmul(ps_deg[:, k, 0:NHALF], zeros16[:, 0:P], zeros16[:, 0:NHALF], start=True, stop=False)
            before_last, nt = load_turns(pe)
            pe.wait_ge(weights_loaded, 16 * 8)

            def turn_half(H, j):
                pe.wait_ge(a_norm, norm_done(H))
                for k in range(2):
                    pe.wait_ge(a_evac, done(H - 1, 2, k))
                    for c in range(HC):
                        mm = pe.transpose(ps_t[:, k, c * P:(c + 1) * P], xn[:, edge_slot(j), k * HC + c, :], ident[:])
                    mm.then_inc(a_turned, 1)

            def hidden_half(H, j):
                pe.wait_ge(a_evac, done(H, 2, 1))
                pe.wait_ge(a_gelu, done(H - 2))
                for k in range(2):
                    mm = pe.matmul(ps_hid[0:HID, j % 2, :], w1_sb[:, k, :],
                                   xn[:, edge_slot(j), k * HC:(k + 1) * HC, :].rearrange("p c f -> p (c f)"),
                                   start=(k == 0), stop=(k == 1))
                mm.then_inc(a_hid, 1)

            def xt_half(H, j):
                pe.wait_ge(a_msg, done(H - 1))
                for c in range(HC):
                    mm = pe.matmul(ps_xt[:, 0, c * F:(c + 1) * F], xn[:, edge_slot(j), c, :], conv_sb[:],
                                   start=True, stop=True)
                mm.then_inc(a_xt, 1)

            def logit_half(H, j):
                pe.wait_ge(a_gelu, done(H))
                pe.wait_ge(a_tanh, done(H - 2))
                for c in range(HC):
                    mm = pe.matmul(ps_z[:, j % 2 * HC + c:j % 2 * HC + c + 1], gel[:, j % 2, c * P:(c + 1) * P],
                                   w2_pair[0:HID, 0:1], start=True, stop=True)
                mm.then_inc(a_z, 1)

            def degree_half(H, j):
                for c in range(HC):
                    pe.wait_ge(a_scaled, H * HC + (c + 1))
                    for part in range(2):
                        for k in range(2):
                            mm = pe.matmul(ps_deg[:, k, 0:NHALF], hot_hi[:, c, part, :],
                                           hot_lo[:, j % 2, c, k * NHALF:(k + 1) * NHALF], start=False, stop=False)
                    mm.then_inc(a_deg, 1)

            def edge_step(turn, j, left):
                H = turn * E + j
                if left >= 0:
                    turn_half(H, j)
                    hidden_half(H, j)
                    xt_half(H, j)
                    logit_half(H, j)
                if j:
                    degree_half(H - 1, j - 1)

            edge_steps(pe, before_last, edge_step)
            for k in range(2):
                mm = pe.matmul(ps_deg[:, k, 0:NHALF], zeros16[:, 0:P], zeros16[:, 0:NHALF], start=False, stop=True)
            mm.then_inc(deg_all, 1)

            xt_banks = (ps_xt[:, 0], ps_deg[:, 1])

            def xt_group(g, s, r, again):
                if not again and g == 0:
                    pe.wait_ge(edges_deg, 1)
                for k in range(2):
                    if again or g >= 1:
                        pe.wait_ge(n_out, g * 2 + (k - 1))
                    for c in range(HJ):
                        mm = pe.matmul(xt_banks[k][:, c * F:(c + 1) * F], xn[:, s, k * HJ + c, :], conv_sb[:],
                                       start=True, stop=True)
                    mm.then_inc(n_xt, 1)

            def turn_group(g, s, r, again):
                pe.wait_ge(n_norm, g + 1)
                for k in range(2):
                    if again or g >= 1:
                        pe.wait_ge(n_evac, g * 2 + (k - 1))
                    for c in range(HJ):
                        mm = pe.transpose(ps_t[:, k, c * P:(c + 1) * P], xn[:, s, k * HJ + c, :], ident[:])
                    mm.then_inc(n_turned, 1)

            def logit_group(g, s, r, again):
                pe.wait_ge(n_gelu, g + 1)
                for c in range(HJ):
                    at = s * J + c
                    mm = pe.matmul(ps_z[:, at:at + HJ + 1:HJ], node_gel[:, c * P:(c + 1) * P], w2_pair[:],
                                   start=True, stop=True)
                mm.then_inc(n_z, 1)

            def hidden_group(g, s, r, again):
                pe.wait_ge(n_evac, g * 2 + 2)
                if again or g >= 1:
                    pe.wait_ge(n_gelu, g)
                for k in range(2):
                    mm = pe.matmul(ps_hid[k * HID:(k + 1) * HID, 0, :], w1_sum[:],
                                   xn[:, s, k * HJ:(k + 1) * HJ, :].rearrange("p c f -> p (c f)"),
                                   start=True, stop=True)
                mm.then_inc(n_hid, 1)

            pipeline(pe, [(turn_group, 3), (logit_group, 4), (xt_group, 4), (hidden_group, 3)])

            def turn_pair(t, b, q):
                if q == 0:
                    pe.wait_ge(s_dst, b + 1)
                pe.wait_ge(s_same, b * Q + (q + 1))
                for k, col in enumerate((dcol, hcol)):
                    for i in range(2):
                        c, at = 2 * q + i, (2 * k + i) * P
                        mm = pe.transpose(ps_t[:, q % 2, at:at + P], col[:, t, c:c + 1].to_broadcast([P, P]),
                                          ident[:])
                mm.then_inc(s_turned, 1)

            def table_pair(b, q):
                pe.wait_ge(s_hot, b * Q + (q + 1))
                for c in (2 * q, 2 * q + 1):
                    pe.wait_ge(s_picked, b * C + (c + 1))
                    for k in range(2):
                        for part_16 in range(2):
                            mm = pe.matmul(table_banks[c % 2][:, k, 0:NHALF], hot_t[:, c % 4, :],
                                           dinv_16[:, part_16, k * NHALF:(k + 1) * NHALF],
                                           start=(part_16 == 0), stop=(part_16 == 1))
                    mm.then_inc(s_table, 1)

            def merge_pair(t, b, q):
                pe.wait_ge(s_same, b * Q + (q + 3))
                if q == 0:
                    pe.wait_ge(s_msg, b + 2)
                a = 2 * q
                pe.wait_ge(s_merged, b * C + (a - 1 + 4))
                pe.matmul(ps_xt[:, 0, 0:F], same[:, q % 2, 0, :], msg_s[:, t, a, :], start=True, stop=False)
                pe.matmul(ps_xt[:, 0, 0:F], same[:, q % 2, 2, :], msg_s[:, t, a + 1, :],
                          start=False, stop=True).then_inc(s_sum, 1)
                pe.wait_ge(s_merged, b * C + (a + 4))
                pe.matmul(ps_xt[:, 1, 0:F], same[:, q % 2, 1, :], msg_s[:, t, a + 1, :],
                          start=True, stop=True).then_inc(s_sum, 1)

            with pe.Fori(0, nt) as turn:
                for t in range(T):
                    b = turn * T + t
                    turn_pair(t, b, 0)
                    for q in range(Q):
                        if q + 1 < Q:
                            turn_pair(t, b, q + 1)
                        table_pair(b, q)
                        merge_pair(t, b, q)

        @block.scalar
        def _(act):
            act.wait_ge(weights_loaded, 16 * 8)
            act.activation(gelu_warm[:], b2_all[:], ACT.Gelu)
            act.activation(b2_half[:], b2_all[:], ACT.Copy, scale=0.5).then_inc(n_warm, 1)
            act.wait_ge(n_warm, 1)
            before_last, nt = load_turns(act)

            def normalise(s, rows=range(J)):
                for c in rows:
                    last = act.activation(xn[:, s, c, :], xin[:, s, c, :], ACT.Relu, bias=shift[:, s, c:c + 1],
                                          scale=rstd[:, s, c:c + 1])
                return last

            def norm_half(H, j, rows):
                if rows[0] == 0:
                    act.wait_ge(a_rstd, done(H))
                    act.wait_ge(a_xt, done(H - 2))
                last = normalise(edge_slot(j), rows)
                if rows[-1] == J - 1:
                    last.then_inc(a_norm, 1)

            def evac_half(H, j):
                for k in range(2):
                    act.wait_ge(a_turned, done(H, 2, k))
                    act.activation(xn[:, edge_slot(j), k * HC:(k + 1) * HC, :].rearrange("p c f -> p (c f)"),
                                   ps_t[:, k, :], ACT.Copy).then_inc(a_evac, 1)

            def gelu_half(H, j):
                act.wait_ge(a_hid, done(H))
                act.wait_ge(a_z, done(H - 2))
                act.activation(gel[:, j % 2, :], ps_hid[0:HID, j % 2, :], ACT.Gelu,
                               bias=b1_col[0:HID, :]).then_inc(a_gelu, 1)

            def tanh_half(H, j):
                act.wait_ge(a_z, done(H))
                act.wait_ge(a_w, done(H - 2))
                act.activation(w_tanh[:, j % 2, :], ps_z[:, j % 2 * HC:(j % 2 + 1) * HC], ACT.Tanh,
                               bias=b2_half[:], scale=0.5).then_inc(a_tanh, 1)

            def message_half(H, j):
                act.wait_ge(a_w, done(H))
                act.wait_ge(a_xt, done(H))
                act.wait_ge(a_xout, done(H - 2))
                for c in range(HC):
                    last = act.activation(xmsg[:, j % 2, c, :], ps_xt[:, 0, c * F:(c + 1) * F], ACT.Copy,
                                          scale=w_col[:, j % 2, c:c + 1])
                last.then_inc(a_msg, 1)

            def scale_hot(H, j):
                act.wait_ge(a_part, H + 1)
                for c in range(HC):
                    act.wait_ge(a_hot, H * HC + (c + 1))
                    act.wait_ge(a_deg, done(H - 1, HC, c))
                    for k in range(2):
                        last = act.activation(hot_hi[:, c, k, :], hot_mask[:, j % 2, c, :], ACT.Copy,
                                              scale=w_part[:, j % 2, k, c:c + 1])
                    last.then_inc(a_scaled, 1)

            def edge_step(turn, j, left):
                H = turn * E + j
                if j:
                    message_half(H - 1, j - 1)
                if left >= 0:
                    evac_half(H, j)
                if j:
                    scale_hot(H - 1, j - 1)
                if left >= 0:
                    gelu_half(H, j)
                if left >= 1:
                    norm_half(H + 1, j + 1, range(0, HC))
                if left >= 0:
                    tanh_half(H, j)
                if left >= 1:
                    norm_half(H + 1, j + 1, range(HC, J))

            norm_half(0, 0, range(J))
            edge_steps(act, before_last, edge_step)

            act.wait_ge(a_xt, done(before_last * E + (E - 1)))
            def norm_group(g, s, r, again):
                act.wait_ge(n_rstd, g + 1)
                normalise(s).then_inc(n_norm, 1)

            def gelu_group(g, s, r, again):
                act.wait_ge(n_hid, g + 1)
                if again or g >= 1:
                    act.wait_ge(n_z, g)
                act.activation(node_gel[:], ps_hid[:, 0, :], ACT.Gelu, bias=b1_col[:]).then_inc(n_gelu, 1)

            def evac_group(g, s, r, again):
                for k in range(2):
                    act.wait_ge(n_turned, g * 2 + (k + 1))
                    act.activation(xn[:, s, k * HJ:(k + 1) * HJ, :].rearrange("p c f -> p (c f)"),
                                   ps_t[:, k, :], ACT.Copy).then_inc(n_evac, 1)

            def tanh_group(g, s, r, again):
                act.wait_ge(n_z, g + 1)
                act.activation(node_tanh[:, s, :], ps_z[:, s * J:(s + 1) * J], ACT.Tanh, bias=b2_half[:],
                               scale=0.5).then_inc(n_tanh, 1)

            pipeline(act, [(evac_group, 3), (tanh_group, 4), (norm_group, 2), (gelu_group, 3)])

            act.wait_ge(c_deg, 1)
            act.activation(dinv[:], deg_rec[:], ACT.Sqrt).then_inc(c_sqrt, 1)

            def scale_messages(turn, t):
                b = turn * T + t
                slot = t % T
                act.wait_ge(s_dinv[slot], turn * (16 * C) + 16 * C * (t // T + 1))
                act.wait_ge(s_msg_in, b * 16 + 16)
                for c in range(C):
                    last = act.activation(msg_s[:, slot, c, :], msg[:, c, :], ACT.Copy,
                                          scale=dinv_src[:, slot, c:c + 1])
                last.then_inc(s_msg, 1)

            scale_messages(0, 0)
            with act.Fori(0, nt) as turn:
                for t in range(T):
                    b = turn * T + t
                    for c in range(C):
                        act.wait_ge(s_sum, b * C + (c + 1 + 4))
                        act.wait_ge(s_picked, b * C + (c + 1 + 2))
                        if c == 0:
                            act.wait_ge(s_landed, b + 1)
                        act.activation(merged[:, t, c, :], ps_xt[:, c % 2, 0:F], ACT.Copy,
                                       scale=dinv_dst[:, t, c:c + 1]).then_inc(s_merged, 1)
                    scale_messages(turn, t + 1)

        @block.vector
        def _(dve):
            def chain(semaphore, base=0):
                count = [0]

                def link(ins):
                    count[0] += 1
                    ins.then_inc(semaphore, 1)
                    dve.wait_ge(semaphore, base + count[0])
                return link, count

            link, _ = chain(prep_vec)
            dve.memset(highest[:, 0:1], 0.0)
            for s, n in credits:
                dve.sem_inc(s, n)
            dve.wait_ge(edges_loaded, 32)
            dve.tensor_copy(src_f[:], src_i[:])
            link(dve.tensor_copy(dst_f[:], dst_i[:]))
            link(dve.tensor_tensor(canon[:], src_f[:], dst_f[:], ALU.is_equal))
            link(dve.scalar_tensor_tensor(loop_dst[:], dst_f[:], 1.0, canon[:], ALU.add, ALU.mult))
            link(dve.tensor_tensor_scan(highest[:, 1:], loop_dst[:], loop_dst[:], 0.0, ALU.max, ALU.max))
            dve.tensor_copy(n_canon[:, 1:2], highest[:, EPP:EPP + 1])
            dve.tensor_copy(n_canon[:, 0:1], highest[:, EPP:EPP + 1]).then_inc(prep_stat, 1)
            dve.wait_ge(prep_pe, 1)
            link(dve.tensor_copy(row2[0:1, 1, :], ps_t[0:1, 0, 0:P]))
            dve.memset(row2[0:1, 0, 0:1], 0.0)
            dve.tensor_tensor_scan(row2[0:1, 0, 1:P], row2[0:1, 1, 0:P - 1], row2[0:1, 1, 0:P - 1], 0.0,
                                   ALU.max, ALU.max).then_inc(carry_ready, 1)
            dve.wait_ge(prep_pe, 2)
            link(dve.tensor_copy(carry[:], ps_t[:, 1, 0:1]))
            link(dve.scalar_tensor_tensor(canon[:], highest[:, 0:EPP], carry[:], loop_dst[:], ALU.max, ALU.is_lt))
            dve.reduce_sum(n_canon[:, 1:2], canon[:], AX_X).then_inc(prep_stat, 1)
            dve.wait_ge(prep_pe, 3)
            link(dve.tensor_scalar(all_canon[:], ps_hid[:, 0, 0:1], float(n_nodes + 1), None, ALU.is_equal))
            link(dve.tensor_scalar(half_canon[:], all_canon[:], 0.5, None, ALU.mult))
            dve.tensor_scalar(half_canon1[:], half_canon[:], 1.0, None, ALU.add)
            dve.wait_ge(pool_const, 14)
            link(dve.tensor_scalar(canon[:], canon[:], all_canon[:], 0.0, ALU.mult, ALU.is_equal))
            link(dve.scalar_tensor_tensor(canon[:], dst_f[:], float(PAD), canon[:], ALU.is_lt, ALU.mult))
            link(dve.tensor_copy(extra[:], canon[:]))
            dve.reduce_sum(n_extra[:], canon[:], AX_X).then_inc(prep_stat, 1)
            link(dve.tensor_scalar(pos_key[:], pos_key[:], VALUE_BITS, None, ALU.logical_shift_left))
            for key, node in ((src_key, src_i), (dst_key, dst_i)):
                link(dve.tensor_tensor(full_key[:], pos_key[:], node[:], ALU.bitwise_or))
                link(dve.copy_predicated(key[:, 0:EPP].bitcast(I32), extra[:], full_key[:]))
            dve.wait_ge(prep_pe, 4)
            link(dve.reduce_max(most[:, 0:1], ps_t[0:1, 0, 0:P], AX_X))
            link(dve.tensor_scalar(n_turns_i[:, 1:2], most[:, 0:1], -1.0, float(T * C), ALU.add, ALU.max))
            dve.tensor_scalar(n_turns_i[:, 0:1], n_turns_i[:, 1:2], (T * C).bit_length() - 1, None,
                              ALU.logical_shift_right).then_inc(turns_known, 1)
            dve.tensor_copy(hi_iota[:], hi_iota_i[:])
            dve.tensor_copy(lo_iota[:], lo_iota_i[:])
            dve.tensor_copy(trash[:], trash_i[:].rearrange("p q c -> p (q c)"))
            dve.tensor_copy(part[:], part_i[:])
            dve.wait_ge(weights_loaded, 16 * 8)
            link(dve.tensor_tensor(w1_sum[:], w1_sb[:, 0, :], w1_sb[:, 1, :], ALU.add))

            before_last, nt = load_turns(dve)

            mask = (1 << VALUE_BITS) - 1

            def sort_max(k):
                return dve.max(best[:, k, :], (src_key, dst_key)[k][:])

            def sort_rest(b, k):
                key, col = ((src_key, src_col), (dst_key, dst_col))[k]
                last = dve.tensor_scalar(col[:, bass.ds(b * C, C)], best[:, k, :].bitcast(I32), mask, None,
                                         ALU.bitwise_and)
                if k:
                    last.then_inc(sorted_block, 1)
                return dve.match_replace(key[:], best[:, k, :], key[:], pad_float)

            def float_dst(b):
                return dve.tensor_scalar(d_f[:], dst_col[:, bass.ds(b * C, C)], 0.0, None, ALU.add)

            def split_dst(b, step):
                cols = bass.ds(b * C, C)
                if step == 0:
                    return dve.tensor_scalar(d_q[:], d_f[:], 1.0 / NPP, 0.5 / NPP - 0.5, ALU.mult, ALU.add)
                if step == 1:
                    return dve.tensor_scalar(d_r[:], d_q[:], ROUND, None, ALU.add)
                if step == 2:
                    return dve.tensor_scalar(d_q[:], d_r[:], ROUND, None, ALU.subtract)
                dve.tensor_copy(hi_col[:, cols], d_q[:])
                return dve.scalar_tensor_tensor(lo_col[:, cols], d_q[:], -float(NPP), d_f[:], ALU.mult, ALU.add)

            MOMENT_LINKS = 4

            def moments(s, link, last):
                link(last)
                dve.tensor_tensor(m_sum[:, s, :], stats[:, s, :, 1], stats[:, s, :, 4], ALU.add)
                dve.tensor_tensor(m2[:, s, :], stats[:, s, :, 2], stats[:, s, :, 5], ALU.add)
                link(dve.tensor_tensor(m_dif[:, s, :], stats[:, s, :, 1], stats[:, s, :, 4], ALU.subtract))
                dve.tensor_scalar(neg_mean[:, s, :], m_sum[:, s, :], -0.5, None, ALU.mult)
                link(dve.tensor_tensor(m_dif[:, s, :], m_dif[:, s, :], m_dif[:, s, :], ALU.mult))
                link(dve.scalar_tensor_tensor(m2[:, s, :], m_dif[:, s, :], F / 4.0, m2[:, s, :], ALU.mult, ALU.add))
                return dve.tensor_scalar(var[:, s, :], m2[:, s, :], 1.0 / F, EPS, ALU.mult, ALU.add)

            LN_LINKS = MOMENT_LINKS + 12

            def one_hot(H, j, c):
                at = H * HC + c
                dve.wait_ge(a_deg, done(H - 2, HC, c))
                dve.tensor_scalar(hot_mask[:, j % 2, c, :], hi_iota[:], hi_col[:, bass.ds(at, 1)], None,
                                  ALU.is_equal)
                dve.tensor_scalar(hot_lo[:, j % 2, c, :], lo_iota[:], lo_col[:, bass.ds(at, 1)], None,
                                  ALU.is_equal).then_inc(a_hot, 1)

            def weight_half(H, j, step):
                h = j % 2
                if step == 0:
                    dve.wait_ge(a_tanh, done(H))
                    dve.wait_ge(a_msg, done(H - 2))
                    dve.tensor_scalar(w_col[:, h, :], w_tanh[:, h, :], 0.5, 0.5, ALU.mult, ALU.add)
                    dve.tensor_scalar(w_scaled[:], w_tanh[:, h, :], W_SCALE / 2, W_SCALE / 2, ALU.mult,
                                      ALU.add).then_inc(a_w, 1)
                elif step == 1:
                    return dve.tensor_copy(w_16[:], w_scaled[:])
                else:
                    dve.tensor_copy(w_part[:, h, 0, :], w_16[:])
                    dve.tensor_tensor(w_part[:, h, 1, :], w_scaled[:], w_16[:],
                                      ALU.subtract).then_inc(a_part, 1)

            def ln_half(turn, j, meanwhile=None):
                H = turn * E + j
                slot = edge_slot(j)
                count = [0]

                def link(ins):
                    ins.then_inc(a_ln, 1)
                    if meanwhile is not None:
                        meanwhile(count[0])
                    count[0] += 1
                    dve.wait_ge(a_ln, H * LN_LINKS + count[0])

                dve.wait_ge(gathered[j % E], turn * (16 * 2 * HC) + 16 * 2 * HC * (j // E + 1))
                for c in range(J):
                    last = dve.bn_stats(stats[:, slot, c, :], xin[:, slot, c, :])
                link(moments(slot, link, last))
                y, v, t = rstd[:, slot, :], var[:, slot, :], m_dif[:, slot, :]
                link(dve.tensor_scalar(y.bitcast(I32), v.bitcast(I32), 1, None, ALU.logical_shift_right))
                dve.tensor_scalar(v, v, -0.5, None, ALU.mult)
                link(dve.tensor_scalar(y.bitcast(I32), y.bitcast(I32), -1.0, float(0x5F3759DF), ALU.mult, ALU.add))
                for _ in range(3):
                    link(dve.tensor_tensor(t, y, y, ALU.mult))
                    link(dve.tensor_tensor(t, t, v, ALU.mult))
                    link(dve.scalar_tensor_tensor(y, t, 1.5, y, ALU.add, ALU.mult))
                dve.tensor_tensor(shift[:, slot, :], neg_mean[:, slot, :], y, ALU.mult).then_inc(a_rstd, 1)
                assert count[0] == LN_LINKS, count[0]

            def edge_step(turn, j, left):
                H = turn * E + j
                k = (j - 1) % 2
                sorted_b = turn * T + ((j - 1) // 2 + LEAD)

                def meanwhile(i):
                    if i == 1 and j:
                        sort_rest(sorted_b, k)
                    if i in (0, 2, 4) and j:
                        weight_half(H - 1, j - 1, i // 2)
                    if j and k:
                        if i == 3:
                            float_dst(sorted_b)
                        if i in (5, 7, 9, 11):
                            split_dst(sorted_b, (i - 5) // 2)
                    if i in (6, 8, 10, 12):
                        one_hot(H, j, (i - 6) // 2)

                if left >= 1:
                    ln_half(turn, j + 1, meanwhile)
                else:
                    weight_half(H - 1, j - 1, 0)
                    dve.wait_ge(a_w, done(H - 1))
                    weight_half(H - 1, j - 1, 1).then_inc(a_rounded, 1)
                    dve.wait_ge(a_rounded, 1 - left)
                    weight_half(H - 1, j - 1, 2)
                    dve.wait_ge(a_part, H)
                    for c in range(HC if left == 0 else 0):
                        one_hot(H, j, c)
                if left >= 2:
                    sort_max(j % 2)

            link, _ = chain(sort_vec)
            for b in range(LEAD):
                for k in range(2):
                    link(sort_max(k))
                    link(sort_rest(b, k))
                link(float_dst(b))
                for step in range(4):
                    link(split_dst(b, step))
            ln_half(0, 0)
            edge_steps(dve, before_last, edge_step)

            def read_degrees():
                dve.wait_ge(deg_all, 1)
                for k in range(2):
                    last = dve.tensor_scalar(deg[:, k * NHALF:(k + 1) * NHALF], ps_deg[:, k, 0:NHALF], 1.0 / W_SCALE,
                                             None, ALU.mult)
                last.then_inc(edges_deg, 1)
                dve.wait_ge(edges_deg, 1)

            COEF_LINKS = 4

            def coef_link(ins, g, i, fill):
                ins.then_inc(n_coef, 1)
                if fill is not None:
                    fill(2 * i)
                    fill(2 * i + 1)
                dve.wait_ge(n_coef, g * COEF_LINKS + (i + 1))

            def node_step(new, old):

                stats_done = None

                def stats_row(c):
                    nonlocal stats_done
                    s = new[1]
                    stats_done = dve.bn_stats(stats[:, s, c, :], xin[:, s, c, :])

                def out_row(t):
                    g, s, _, _ = old
                    k, c = t // HJ, t % HJ
                    if t == 0:
                        dve.wait_ge(n_bias, g + 1)
                    if c == 0:
                        dve.wait_ge(n_xt, g * 2 + (k + 1))
                    bank = (ps_xt[:, 0], ps_deg[:, 1])[k]
                    last = dve.scalar_tensor_tensor(xin[:, s, t, :], bank[:, c * F:(c + 1) * F], coef[:, s, t:t + 1],
                                                    xin[:, s, t, :], ALU.mult, ALU.add)
                    if c == HJ - 1:
                        last.then_inc(n_out, 1)

                if new is not None:
                    dve.wait_ge(n_loaded[new[1]], new[2] * 16 + 16)
                if old is not None:
                    g, s, _, again = old
                    if not again and g == 0:
                        read_degrees()
                    fill = None if new is None else stats_row
                    cols = bass.ds(g * J, J)
                    dve.wait_ge(n_tanh, g + 1)
                    coef_link(dve.tensor_scalar(self_w[:, s, :], node_tanh[:, s, :], half_canon[:], half_canon1[:],
                                                ALU.mult, ALU.add), g, 0, fill)
                    coef_link(dve.tensor_tensor(deg[:, cols], deg[:, cols], self_w[:, s, :], ALU.add), g, 1, fill)
                    dve.scalar_tensor_tensor(self_w[:, s, :], deg[:, cols], 0.0, self_w[:, s, :],
                                             ALU.is_gt, ALU.mult)
                    coef_link(dve.reciprocal(deg_rec[:, cols], deg[:, cols]), g, 2, fill)
                    coef_link(dve.tensor_tensor(coef[:, s, :], self_w[:, s, :], deg_rec[:, cols], ALU.mult), g, 3,
                              fill)
                elif new is not None:
                    for c in range(J):
                        stats_row(c)
                if new is not None:
                    g, s, _, _ = new
                    count = [0]

                    def link(ins):
                        ins.then_inc(n_vec, 1)
                        if old is not None:
                            out_row(2 * count[0])
                            out_row(2 * count[0] + 1)
                        count[0] += 1
                        dve.wait_ge(n_vec, g * MOMENT_LINKS + count[0])

                    moments(s, link, stats_done).then_inc(n_var, 1)
                    assert count[0] == MOMENT_LINKS and 2 * MOMENT_LINKS == J
                elif old is not None:
                    for t in range(J):
                        out_row(t)

            pipeline(dve, [(node_step, 0, 4)])

            for t in range(T):
                dve.tensor_copy(dinv_idx[:, t, :], src_col[:, t * C:(t + 1) * C]).then_inc(s_idx, 1)
            link, _ = chain(c_vec)
            dve.sem_inc(c_deg, 1)
            dve.wait_ge(c_sqrt, 1)
            link(dve.tensor_tensor(t_b[:], dinv[:], dinv[:], ALU.mult))
            link(dve.tensor_tensor(t_b[:], t_b[:], deg[:], ALU.mult))
            link(dve.tensor_scalar(t_b[:], t_b[:], -0.5, 1.5, ALU.mult, ALU.add))
            link(dve.tensor_tensor(dinv[:], dinv[:], t_b[:], ALU.mult))
            dve.scalar_tensor_tensor(dinv[:], deg[:], 0.0, dinv[:], ALU.is_gt, ALU.mult).then_inc(c_dinv, 1)
            dve.wait_ge(c_dinv, 1)
            link(dve.tensor_scalar(t_b[:], dinv[:], W_SCALE, None, ALU.mult))
            link(dve.tensor_copy(dinv_16[:, 0, :], t_b[:]))
            link(dve.tensor_tensor(dinv_16[:, 1, :], t_b[:], dinv_16[:, 0, :], ALU.subtract))

            S_LINKS = 3
            lo_halves = lo_iota[:].rearrange("p (k n) -> p k n", k=2)

            def copy_columns(t, b):
                cols = bass.ds(b * C, C)
                dve.tensor_copy(lcol[:, t % T, :], lo_col[:, cols])
                dve.tensor_copy(hcol[:, t % T, :], hi_col[:, cols])
                dve.tensor_copy(dcol[:, t % T, :], dst_col[:, cols]).then_inc(s_dst, 1)

            def compare_pair(t, b, q):
                a = 2 * q
                dve.wait_ge(s_turned, b * Q + (q + 1))
                for c in (a, a + 1):
                    last = dve.tensor_scalar(hot_t[:, c % 4, :],
                                             ps_t[:, q % 2, (2 + c % 2) * P:(3 + c % 2) * P], part[:],
                                             1.0 / W_SCALE, ALU.is_equal, ALU.mult)
                last.then_inc(s_hot, 1)
                dve.wait_ge(s_sum, b * C + (a + 2))
                for k, (col, row) in enumerate(((0, 0), (1, 1), (1, 0))):
                    last = dve.tensor_scalar(same[:, q % 2, k, :], ps_t[:, q % 2, row * P:(row + 1) * P],
                                             dcol[:, t, a + col:a + col + 1], None, ALU.is_equal)
                last.then_inc(s_same, 1)
                dve.wait_ge(s_same, b * Q + (q + 3))
                dve.tensor_tensor_reduce(same_a[:], same[:, q % 2, 0, :], lower[:, 0:P], 1.0, 0.0, ALU.mult,
                                         ALU.add, prior[:, a:a + 1])
                return dve.tensor_tensor_reduce(same_b[:], same[:, q % 2, 1:3, :].rearrange("p k f -> p (k f)"),
                                                lower[:], 1.0, 0.0, ALU.mult, ALU.add, prior[:, a + 1:a + 2])

            def pick_pair(t, b, q):
                for c in (2 * q, 2 * q + 1):
                    dve.wait_ge(s_table, b * C + (c + 1))
                    dve.wait_ge(s_picked, b * C + (c + 1))
                    dve.scalar_tensor_tensor(picked[:, c % 2], lo_halves, lcol[:, t, c:c + 1],
                                             table_banks[c % 2][:, :, 0:NHALF], ALU.is_equal, ALU.mult,
                                             accum_out=dinv_dst[:, t, c:c + 1]).then_inc(s_picked, 1)

            copy_columns(0, 0)
            dve.wait_ge(s_dst, 1)
            with dve.Fori(0, nt) as turn:
                for t in range(T):
                    b = turn * T + t
                    link, n = chain(s_vec, b * S_LINKS)
                    for q in range(Q):
                        last = compare_pair(t, b, q)
                        if q >= 1:
                            pick_pair(t, b, q - 1)
                    link(last)
                    copy_columns(t + 1, b + 1)
                    pick_pair(t, b, Q - 1)
                    link(dve.tensor_tensor(to_trash[:], trash[:], dcol[:, t, :], ALU.subtract))
                    link(dve.scalar_tensor_tensor(row_f[:], prior[:], 0.0, to_trash[:], ALU.is_gt, ALU.mult))
                    dve.wait_ge(s_landed, b + 1)
                    dve.tensor_tensor(row_idx[:, t, :], row_f[:], dcol[:, t, :], ALU.add).then_inc(s_row, 1)
                    dve.wait_ge(s_msg, b + 2)
                    dve.tensor_copy(dinv_idx[:, t, :], src_col[:, bass.ds(b * C + T * C, C)]).then_inc(s_idx, 1)
                    dve.wait_ge(s_row, b + 1)
                    assert n[0] == S_LINKS


def kernel(x, src, dst, L0_gnn_mlp_w1, L0_gnn_mlp_b1, L0_gnn_mlp_w2, L0_gnn_mlp_b2, L0_gnn_conv_w, L0_gnn_conv_b):
    import numpy as np
    import concourse.bacc as bacc
    from concourse.bass_utils import run_bass_kernel_spmd

    x = np.asarray(x)
    n_nodes, n_edges = x.shape[0], np.asarray(src).shape[0]
    npp, epp = sizes(n_nodes, n_edges)
    arrays = {
        "x": np.zeros((P * npp, F), np.float32),
        "src": np.full(P * epp, n_nodes, np.int32),
        "dst": np.full(P * epp, n_nodes, np.int32),
    }
    arrays["x"][:n_nodes] = x
    arrays["src"][:n_edges] = np.asarray(src)
    arrays["dst"][:n_edges] = np.asarray(dst)
    arrays["src"] = arrays["src"].reshape(P, epp)
    arrays["dst"] = arrays["dst"].reshape(P, epp)
    arrays["w1"] = np.ascontiguousarray(L0_gnn_mlp_w1)
    arrays["b1"] = np.asarray(L0_gnn_mlp_b1).reshape(HID, 1)
    arrays["w2"] = np.asarray(L0_gnn_mlp_w2).reshape(HID, 1)
    arrays["b2"] = np.asarray(L0_gnn_mlp_b2).reshape(1, 1)
    arrays["conv_w"] = np.ascontiguousarray(L0_gnn_conv_w)
    arrays["conv_b"] = np.asarray(L0_gnn_conv_b).reshape(1, F)

    nc = bacc.Bacc("TRN2", target_bir_lowering=False, num_devices=1)
    aps = [nc.dram_tensor(f"in_{n}", a.shape, mybir.dt.from_np(a.dtype), kind="ExternalInput").ap()
           for n, a in arrays.items()]
    out = nc.dram_tensor("out", (P * npp, F), F32, kind="ExternalOutput").ap()
    gnn_layer(nc, n_nodes, *aps, out)
    r = run_bass_kernel_spmd(nc, [{f"in_{n}": a for n, a in arrays.items()}], core_ids=[0])
    return r.results[0]["out"][:n_nodes]
```
